# Optimizing a Trainium2 kernel written in Bass

```python
import numpy as np
import jax
import jax.numpy as jnp

def _softmax(x, axis=-1):
    return jax.nn.softmax(x, axis=axis)

def _gelu(x):
    return jax.nn.gelu(x, approximate=True)

def _silu(x):
    return jax.nn.silu(x)

def _sigmoid(x):
    return jax.nn.sigmoid(x)

def _layernorm(x, axis=-1, eps=1e-05):
    m = jnp.mean(x, axis=axis, keepdims=True)
    v = jnp.var(x, axis=axis, keepdims=True)
    return (x - m) / jnp.sqrt(v + eps)

def _scatter_add(tgt, idx, src, axis=0):
    return tgt.at[idx].add(src)

def _segment_sum(src, seg, n):
    return jax.ops.segment_sum(src, seg, n)
kernel_name = 'mk_xattn_ffn_d1_seqx_r8_37946d'

def setup_inputs(seed: int=0):
    np.random.seed(seed)
    _w = jnp.asarray

    def _rec_inputs():
        import jax
        import jax.numpy as jnp
        _rk = jax.random.key(seed)
        x = 7.22e-05 + 1 * jax.random.normal(jax.random.fold_in(_rk, 1), (32, 64, 128), jnp.float32)
        _lenS = 64 - jax.random.randint(jax.random.fold_in(_rk, 7), (32,), 0, max(1, 64 // 4) + 1, jnp.int32)
        _lenS2 = 64 - jax.random.randint(jax.random.fold_in(_rk, 8), (32,), 0, max(1, 64 // 4) + 1, jnp.int32)
        _ctx_1024P = jax.random.normal(jax.random.fold_in(_rk, 11), (32, 16, 128), jnp.float32)
        _ctx_1024c = jax.random.dirichlet(jax.random.fold_in(_rk, 511), 0.3 * jnp.ones((16,), jnp.float32), (32, 64))
        _ctx_1024t = jnp.einsum('bsk,bkd->bsd', _ctx_1024c, _ctx_1024P)
        _ctx_1024t = _ctx_1024t * jax.lax.rsqrt(jnp.mean(jnp.square(_ctx_1024t)) + 1e-12) * 0.953939
        ctx_1024 = 4.13588e-05 + 0.999923 * (_ctx_1024t + 0.3 * jax.random.normal(jax.random.fold_in(_rk, 611), (32, 64, 128), jnp.float32))
        return (x, ctx_1024)
    x, ctx_1024 = _rec_inputs()

    def _L0_xattn_setup():
        import jax, jax.numpy as jnp
        import numpy as np
        import math
        EMBED_DIM = 128
        NUM_HEADS = 16
        HEAD_DIM = EMBED_DIM // NUM_HEADS
        key = jax.random.key(seed)
        ks = jax.random.split(key, 11)
        B, S, D = (4, 256, EMBED_DIM)
        scale = 1.0 / math.sqrt(D)
        inp = {'q': jax.random.normal(ks[0], (B, S, D), dtype=jnp.float32), 'k': jax.random.normal(ks[1], (B, S, D), dtype=jnp.float32), 'v': jax.random.normal(ks[2], (B, S, D), dtype=jnp.float32), 'Wq': jax.random.normal(ks[3], (D, D), dtype=jnp.float32) * scale, 'bq': jnp.zeros((D,), dtype=jnp.float32), 'Wk': jax.random.normal(ks[4], (D, D), dtype=jnp.float32) * scale, 'bk': jnp.zeros((D,), dtype=jnp.float32), 'Wv': jax.random.normal(ks[5], (D, D), dtype=jnp.float32) * scale, 'bv': jnp.zeros((D,), dtype=jnp.float32), 'Wo': jax.random.normal(ks[6], (D, D), dtype=jnp.float32) * scale, 'bo': jnp.zeros((D,), dtype=jnp.float32)}
        return inp
    _L0_xattn_all = _L0_xattn_setup()
    _L0_xattn_in = {k: v for k, v in _L0_xattn_all.items() if k in ('Wq', 'bq', 'Wk', 'bk', 'Wv', 'bv', 'Wo', 'bo')}
    del _L0_xattn_all

    def _L0_ffn_setup():
        import jax, jax.numpy as jnp
        import numpy as np
        B, S, H = (8, 128, 128)
        FF = 512
        E = 8
        TOP_K = 2
        LN_EPS = 1e-12

        def _layernorm(x, w, b):
            mu = jnp.mean(x, axis=-1, keepdims=True)
            var = jnp.mean(jnp.square(x - mu), axis=-1, keepdims=True)
            return (x - mu) * jax.lax.rsqrt(var + LN_EPS) * w + b
        key = jax.random.key(seed)
        ks = jax.random.split(key, 8)
        sc_h = 1.0 / np.sqrt(H)
        sc_ff = 1.0 / np.sqrt(FF)
        return {'hidden_states': jax.random.normal(ks[0], (B, S, H), jnp.float32), 'router_w': jax.random.normal(ks[1], (E, H), jnp.float32) * sc_h, 'router_b': jnp.zeros((E,), jnp.float32), 'w1': jax.random.normal(ks[2], (E, FF, H), jnp.float32) * sc_h, 'b1': jax.random.normal(ks[3], (E, FF), jnp.float32) * 0.01, 'w2': jax.random.normal(ks[4], (E, H, FF), jnp.float32) * sc_ff, 'b2': jax.random.normal(ks[5], (E, H), jnp.float32) * 0.01, 'ln_w': jnp.ones((H,), jnp.float32), 'ln_b': jnp.zeros((H,), jnp.float32)}
    _L0_ffn_all = _L0_ffn_setup()
    _L0_ffn_in = {k: v for k, v in _L0_ffn_all.items() if k in ('router_w', 'router_b', 'w1', 'b1', 'w2', 'b2', 'ln_w', 'ln_b')}
    del _L0_ffn_all
    return {'x': x, 'ctx_1024': ctx_1024, 'L0_xattn_Wq': _L0_xattn_in['Wq'], 'L0_xattn_bq': _L0_xattn_in['bq'], 'L0_xattn_Wk': _L0_xattn_in['Wk'], 'L0_xattn_bk': _L0_xattn_in['bk'], 'L0_xattn_Wv': _L0_xattn_in['Wv'], 'L0_xattn_bv': _L0_xattn_in['bv'], 'L0_xattn_Wo': _L0_xattn_in['Wo'], 'L0_xattn_bo': _L0_xattn_in['bo'], 'L0_ffn_router_w': _L0_ffn_in['router_w'], 'L0_ffn_router_b': _L0_ffn_in['router_b'], 'L0_ffn_w1': _L0_ffn_in['w1'], 'L0_ffn_b1': _L0_ffn_in['b1'], 'L0_ffn_w2': _L0_ffn_in['w2'], 'L0_ffn_b2': _L0_ffn_in['b2'], 'L0_ffn_ln_w': _L0_ffn_in['ln_w'], 'L0_ffn_ln_b': _L0_ffn_in['ln_b']}

def reference(x, ctx_1024, L0_xattn_Wq, L0_xattn_bq, L0_xattn_Wk, L0_xattn_bk, L0_xattn_Wv, L0_xattn_bv, L0_xattn_Wo, L0_xattn_bo, L0_ffn_router_w, L0_ffn_router_b, L0_ffn_w1, L0_ffn_b1, L0_ffn_w2, L0_ffn_b2, L0_ffn_ln_w, L0_ffn_ln_b):
    import jax
    import jax.numpy as jnp

    def _L0_xattn_ref(q, k, v, Wq, bq, Wk, bk, Wv, bv, Wo, bo):
        import jax, jax.numpy as jnp
        import numpy as np
        import math
        EMBED_DIM = 128
        NUM_HEADS = 16
        HEAD_DIM = EMBED_DIM // NUM_HEADS
        B, S, D = q.shape
        H, Hd = (NUM_HEADS, HEAD_DIM)
        qh = (q @ Wq.T + bq).reshape(B, S, H, Hd).transpose(0, 2, 1, 3)
        kh = (k @ Wk.T + bk).reshape(B, S, H, Hd).transpose(0, 2, 1, 3)
        vh = (v @ Wv.T + bv).reshape(B, S, H, Hd).transpose(0, 2, 1, 3)
        scores = jnp.einsum('bhqd,bhkd->bhqk', qh, kh) / math.sqrt(Hd)
        probs = jax.nn.softmax(scores, axis=-1)
        attn = jnp.einsum('bhqk,bhkd->bhqd', probs, vh)
        concat = attn.transpose(0, 2, 1, 3).reshape(B, S, D)
        return concat @ Wo.T + bo

    def _L0_ffn_ref(hidden_states, router_w, router_b, w1, b1, w2, b2, ln_w, ln_b):
        import jax, jax.numpy as jnp
        import numpy as np
        B, S, H = (8, 128, 128)
        FF = 512
        E = 8
        TOP_K = 2
        LN_EPS = 1e-12

        def _layernorm(x, w, b):
            mu = jnp.mean(x, axis=-1, keepdims=True)
            var = jnp.mean(jnp.square(x - mu), axis=-1, keepdims=True)
            return (x - mu) * jax.lax.rsqrt(var + LN_EPS) * w + b
        b, s, h = hidden_states.shape
        flat = hidden_states.reshape(-1, h)
        logits = flat @ router_w.T + router_b
        topk_vals, topk_idx = jax.lax.top_k(logits, TOP_K)
        topk_w = jax.nn.softmax(topk_vals, axis=-1)
        out = jnp.zeros_like(flat)
        n_exp = w1.shape[0]
        for e in range(n_exp):
            cw = jnp.sum(jnp.where(topk_idx == e, topk_w, 0.0), axis=-1)
            y = jax.nn.gelu(flat @ w1[e].T + b1[e], approximate=False)
            y = y @ w2[e].T + b2[e]
            out = out + y * cw[:, None]
        out = out.reshape(b, s, h) + hidden_states
        return _layernorm(out, ln_w, ln_b)
    x = x + _L0_xattn_ref(_layernorm(x, axis=-1), ctx_1024, ctx_1024, L0_xattn_Wq, L0_xattn_bq, L0_xattn_Wk, L0_xattn_bk, L0_xattn_Wv, L0_xattn_bv, L0_xattn_Wo, L0_xattn_bo)
    x = x + _L0_ffn_ref(_layernorm(x, axis=-1), L0_ffn_router_w, L0_ffn_router_b, L0_ffn_w1, L0_ffn_b1, L0_ffn_w2, L0_ffn_b2, L0_ffn_ln_w, L0_ffn_ln_b)
    return x

_drawn_inputs = setup_inputs


def setup_inputs(seed=0):
    import zlib

    import numpy as np

    out = dict(_drawn_inputs(seed))
    spreads = {'L0_xattn_bq': (0.0, 0.1),
     'L0_xattn_bk': (0.0, 2.0),
     'L0_xattn_bv': (0.0, 0.1),
     'L0_xattn_bo': (0.0, 0.1),
     'L0_ffn_router_b': (0.0, 0.1),
     'L0_ffn_ln_w': (1.0, 0.2),
     'L0_ffn_ln_b': (0.0, 0.1)}
    factors = {'L0_ffn_b1': 25.265, 'L0_ffn_b2': 8.0}
    for name, (base, spread) in spreads.items():
        noise = np.random.default_rng([zlib.crc32(name.encode()), seed]).standard_normal(out[name].shape)
        drawn = base * np.exp(spread * noise) if base else spread * noise
        out[name] = jnp.asarray(drawn.astype(out[name].dtype))
    for name, factor in factors.items():
        out[name] = (out[name] * factor).astype(out[name].dtype)
    return out
```

```python
from contextlib import ExitStack

import concourse.bass as bass
from concourse import mybir

ALU = mybir.AluOpType
ACT = mybir.ActivationFunctionType
AX = mybir.AxisListType
F32 = mybir.dt.float32
F16 = mybir.dt.float16
BF16 = mybir.dt.bfloat16

P = 128
D = 128
HEADS = 16
HD = D // HEADS
BATCH, SEQ = 32, 64
TOKENS = BATCH * SEQ
PAIRS = TOKENS // P
SLOTS = 3
STAGES = 4
EXPERTS = 8
FF = 512
FC = FF // P
BLOCKS = TOKENS // 512
BT = 512 // P
EPS_OUT = 1e-12
WARM = 10
CHUNK = 4
SCALE = float(HD) ** -0.5
EPS_IN = 1e-5


def attention(nc, x1, w_hi, w_lo, x, ctxT, w4, consts, bo, w_ffn):
    with ExitStack() as stack:
        def sb(name, shape, dt=F32):
            return stack.enter_context(nc.sbuf_tensor(name, shape, dt))

        def pb(name, shape, dt=F32):
            return stack.enter_context(nc.psum_tensor(name, shape, dt))

        def sem(name):
            return stack.enter_context(nc.semaphore(name))

        x_sb = sb("x_sb", [P, PAIRS, D])
        x_res = sb("x_res", [P, PAIRS, D])
        w_raw = sb("w_raw", [P, 2 * EXPERTS, 512])
        ctx_sb = [sb(f"ctx{i}", [P, P]) for i in range(SLOTS)]
        w = sb("w", [P, 4, D])
        cst = sb("cst", [P, P + 11])
        id32, mh, mm, b_col = cst[:, 0:P], cst[:, P:P + 4], cst[:, P + 4:P + 8], cst[:, P + 8:P + 11]
        bq_s = sb("bq_s", [P, 1])
        bo_row = sb("bo_row", [P, D])
        bv_mat = sb("bv_mat", [P, P])
        bvo = sb("bvo", [P, D])
        id16 = sb("id16", [P, P], F16)
        sel = sb("sel", [P, 4, 4, 96], F16)
        stats = sb("stats", [P, PAIRS, 6])
        mv = sb("mv", [P, PAIRS, 2])
        half = sb("half", [P, PAIRS])
        veps = sb("veps", [P, PAIRS])
        rstd = sb("rstd", [P, PAIRS])
        nmr = sb("nmr", [P, PAIRS])
        nmean = sb("nmean", [P, PAIRS])
        xh = [sb(f"xh{i}", [P, D]) for i in range(SLOTS)]
        xr = [sb(f"xr{i}", [P, D]) for i in range(SLOTS)]
        cols = [sb(f"cols{i}", [P, 2, P]) for i in range(SLOTS)]
        qk = [sb(f"qk{i}", [P, 2, P]) for i in range(SLOTS)]
        qk_hi = [sb(f"qk_hi{i}", [P, 2, P], F16) for i in range(SLOTS)]
        qk_lo = [sb(f"qk_lo{i}", [P, 2, P], F16) for i in range(SLOTS)]
        kbd = [sb(f"kbd{i}", [P, 4, P], F16) for i in range(SLOTS)]
        q_stack = [sb(f"q_stack{i}", [P, 4, P], F16) for i in range(SLOTS)]
        k_stack = [sb(f"k_stack{i}", [P, 4, P], F16) for i in range(SLOTS)]
        qbd = [sb(f"qbd{i}", [P, 4, 4, P], F16) for i in range(SLOTS)]
        vbd = [sb(f"vbd{i}", [P, 2, 8, 17]) for i in range(SLOTS)]
        nmax = [sb(f"nmax{i}", [P, 4, 32], F16) for i in range(SLOTS)]
        pT = [sb(f"pT{i}", [P, 4, 256]) for i in range(SLOTS)]
        rden = [sb(f"rden{i}", [P, 8, 2]) for i in range(SLOTS)]
        att = [sb(f"att{i}", [P, 8, 2, HD]) for i in range(SLOTS)]

        psS = pb("psS", [P, 2, 512])
        psT = pb("psT", [P, 2, 512])
        psR = [pb("psRq", [P, 4, P]), pb("psRk", [P, 4, P])]
        psA = pb("psA", [P, 512])
        psV = pb("psV", [P, 512])

        act_warm = sb("act_warm", [P, 1])
        warm = sb("warm", [P, 512], BF16)
        warm_ready = sem("warm_ready")
        x_in = [sem(f"x_in{c}") for c in range(PAIRS // CHUNK)]
        wraw_in = [sem(f"wraw_in{i}") for i in range(4)]
        hi_split = sem("hi_split")
        lo_split = sem("lo_split")
        ctx_in = sem("ctx_in")
        w_in = sem("w_in")
        c_in = sem("c_in")
        const_ready = sem("const_ready")
        pool_const = sem("pool_const")
        stats_raw = sem("stats_raw")
        stats_ready = sem("stats_ready")
        rs = sem("rs")
        bvo_ps = sem("bvo_ps")
        bvo_sb = sem("bvo_sb")
        res_ready = sem("res_ready")
        xh_ready = sem("xh_ready")
        xr_ready = sem("xr_ready")
        colsT = sem("colsT")
        cols_sb = sem("cols_sb")
        qkv_ps = sem("qkv_ps")
        qkv_sb = sem("qkv_sb")
        bd_ready = sem("bd_ready")
        s_ps = sem("s_ps")
        max_ready = sem("max_ready")
        mT_ps = sem("mT_ps")
        rep_ps = sem("rep_ps")
        rep_sb = sem("rep_sb")
        mT_sb = sem("mT_sb")
        qbd_ready = sem("qbd_ready")
        hi_ready = sem("hi_ready")
        t_ps = sem("t_ps")
        exp_ready = sem("exp_ready")
        pv_ps = sem("pv_ps")
        rden_ready = sem("rden_ready")
        att_ready = sem("att_ready")
        out_done = sem("out_done")

        x_t = x.rearrange("(t p) d -> p t d", p=P)

        block = stack.enter_context(nc.Block())

        def steps(engine, step):
            for v in range(STAGES):
                step(v, v)
            with engine.Fori(0, (PAIRS - STAGES) // SLOTS) as i:
                for k in range(SLOTS):
                    step(i * SLOTS + (STAGES + k), STAGES + k, True)
            for v in range(PAIRS, PAIRS + STAGES):
                step(v, v)

        def runs(v0, lag, steady):
            return steady or 0 <= v0 - lag < PAIRS

        @block.sync
        def _(sp):
            sp.dma_start(x_sb[:, 0:CHUNK, :], x_t[:, 0:CHUNK, :]).then_inc(x_in[0], 16)
            sp.dma_start(w[:], w4).then_inc(w_in, 16)
            sp.dma_start(ctx_sb[0][:], ctxT[:, 0:P]).then_inc(ctx_in, 16)
            for c in range(1, PAIRS // CHUNK):
                sp.dma_start(x_sb[:, c * CHUNK:(c + 1) * CHUNK, :],
                             x_t[:, c * CHUNK:(c + 1) * CHUNK, :]).then_inc(x_in[c], 16)
            for v in range(1, PAIRS):
                sp.wait_ge(ctx_in, 16 * v)
                if v >= SLOTS:
                    sp.wait_ge(qkv_ps, v - SLOTS + 1)
                sp.dma_start(ctx_sb[v % SLOTS][:], ctxT[:, v * P:(v + 1) * P]).then_inc(ctx_in, 16)
                if v == 2:
                    for i in range(4):
                        sp.dma_start(w_raw[:, 4 * i:4 * i + 4, :], w_ffn[:, 4 * i:4 * i + 4, :]).then_inc(wraw_in[i], 16)

        @block.gpsimd
        def _(pool):
            g = nc.gpsimd
            g.memset(half[:], -0.5).then_inc(pool_const, 1)
            for i in range(SLOTS):
                g.memset(vbd[i][:], 0.0).then_inc(pool_const, 1)
                g.memset(nmax[i][:], 0.0).then_inc(pool_const, 1)
            pool.wait_ge(pool_const, 1 + 2 * SLOTS)
            for i in range(SLOTS):
                g.memset(k_stack[i][96:P], 1.0).then_inc(pool_const, 1)
            pool.wait_ge(pool_const, 1 + 3 * SLOTS)
            for i in range(SLOTS):
                for b in range(2):
                    g.memset(vbd[i][64 * b:64 * b + 64, b, :, 16:17], 1.0).then_inc(pool_const, 1)
            pool.wait_ge(pool_const, 1 + 5 * SLOTS)
            def rstd_of(c):
                t = slice(c * CHUNK, (c + 1) * CHUNK)
                pool.wait_ge(stats_ready, (c + 1) * CHUNK)
                g.tensor_scalar(veps[:, t], mv[:, t, 1], EPS_IN, 1.0, ALU.add, ALU.mult).then_inc(rs, 1)
                g.tensor_scalar(nmean[:, t], mv[:, t, 0], -1.0, 1.0, ALU.mult, ALU.mult).then_inc(rs, 1)
                pool.wait_ge(rs, 4 * c + 2)
                g.tensor_tensor(rstd[:, t], veps[:, t], half[:, t], ALU.pow).then_inc(rs, 1)
                pool.wait_ge(rs, 4 * c + 3)
                g.tensor_tensor(nmr[:, t], nmean[:, t], rstd[:, t], ALU.mult).then_inc(rs, 1)
                pool.wait_ge(rs, 4 * c + 4)

            def normalise(v, s, reused):
                at = bass.ds(v, 1)
                g.tensor_tensor(xr[s][:], x_sb[:, at, :].rearrange("p a d -> p (a d)"),
                                rstd[:, at].to_broadcast([P, D]), ALU.mult).then_inc(xr_ready, 1)
                if reused:
                    pool.wait_ge(colsT, v - (SLOTS - 1))
                    pool.nop()
                pool.wait_ge(xr_ready, v + 1)
                pool.nop()
                g.tensor_tensor(xh[s][:], xr[s][:], nmr[:, at].to_broadcast([P, D]), ALU.add).then_inc(xh_ready, 1)

            def residual(v):
                at = bass.ds(v, 1)
                g.tensor_tensor(x_res[:, at, :].rearrange("p a d -> p (a d)"),
                                x_sb[:, at, :].rearrange("p a d -> p (a d)"), bvo[:], ALU.add).then_inc(res_ready, 1)

            def low_part(v):
                at = bass.ds(v, 1)
                pool.wait_ge(hi_split, v + 1)
                pool.nop()
                g.tensor_tensor(w_lo[:, at, :].rearrange("p a d -> p (a d)"),
                                w_raw[:, at, :].rearrange("p a d -> p (a d)"),
                                w_hi[:, at, :].rearrange("p a d -> p (a d)"), ALU.subtract).then_inc(lo_split, 1)

            rstd_of(0)
            for v in range(SLOTS):
                normalise(v, v, False)
            for c in range(1, PAIRS // CHUNK):
                rstd_of(c)
            normalise(SLOTS, 0, True)
            pool.wait_ge(bvo_sb, 1)
            with pool.Fori(0, (PAIRS - STAGES) // SLOTS) as i:
                for k in range(SLOTS):
                    residual(i * SLOTS + k)
                    normalise(i * SLOTS + (STAGES + k), (STAGES + k) % SLOTS, True)
                    low_part(i * SLOTS + k)
            for v in range(PAIRS - STAGES, PAIRS):
                residual(v)
                low_part(v)

        @block.vector
        def _(dve):
            v_ = nc.vector
            v_.memset(warm[:], 0.0).then_inc(warm_ready, 1)

            def chunk_stats(c):
                dve.wait_ge(x_in[c], 16)
                for t in range(c * CHUNK, (c + 1) * CHUNK):
                    v_.bn_stats(stats[:, t, :], x_sb[:, t, :]).then_inc(stats_raw, 1)
                for t in range(c * CHUNK, (c + 1) * CHUNK):
                    dve.wait_ge(stats_raw, t + 1)
                    v_.bn_aggr(mv[:, t, :], stats[:, t, :]).then_inc(stats_ready, 1)

            chunk_stats(0)
            dve.wait_ge(c_in, 32)
            v_.tensor_copy(id16[:], id32).then_inc(const_ready, 1)
            v_.memset(sel[:], 0.0).then_inc(const_ready, 1)
            v_.memset(bv_mat[:], 1.0).then_inc(const_ready, 1)
            v_.tensor_scalar(bq_s[:], b_col[:, 0:1], SCALE, None, ALU.mult).then_inc(const_ready, 1)
            dve.wait_ge(const_ready, 4)
            for i, blocks in enumerate(((0, 2), (1,), (0, 1), (2,))):
                for k in blocks:
                    v_.tensor_copy(sel[:, i, :, 32 * k:32 * k + 32],
                                   id16[:].rearrange("p (g c) -> p g c", g=4)).then_inc(const_ready, 1)
            v_.tensor_scalar(bv_mat[:], bv_mat[:], b_col[:, 2:3], None, ALU.mult).then_inc(const_ready, 1)
            dve.wait_ge(bvo_ps, 1)
            v_.tensor_tensor(bvo[:], psV[:, 0:D], bo_row[:], ALU.add).then_inc(bvo_sb, 1)
            for c in range(1, PAIRS // CHUNK):
                chunk_stats(c)

            def step(v, v0, steady=False):
                s = v0 % SLOTS
                s1, s2, s3 = (v0 - 1) % SLOTS, (v0 - 2) % SLOTS, (v0 - 3) % SLOTS

                def largest(h):
                    dve.wait_ge(s_ps, 2 * v - 1 + h)
                    v_.tensor_reduce(nmax[s1][:, 2 * h:2 * h + 2, 0:4],
                                     psS[:, :, 0:256].rearrange("p g (h k) -> p g h k", h=4),
                                     AX.X, ALU.max, negate=True).then_inc(max_ready, 1)

                if runs(v0, 1, steady):
                    largest(0)
                if runs(v0, 2, steady):
                    dve.wait_ge(mT_sb, v - 1)
                    for j in range(4):
                        last = v_.tensor_scalar(qbd[s2][:, :, j, :], q_stack[s2][:], mm[:, j:j + 1], None, ALU.mult)
                    last.then_inc(qbd_ready, 1)
                if runs(v0, 3, steady) or runs(v0, 4, steady):
                    dve.wait_ge(pv_ps, v - 2)
                if runs(v0, 3, steady):
                    pv = psV[:, P:P + 272].rearrange("p (h b c) -> p h b c", h=8, b=2)
                    v_.reciprocal(rden[s3][:], pv[:, :, :, 16]).then_inc(rden_ready, 1)
                if runs(v0, 4, steady):
                    dve.wait_ge(res_ready, v - 3)
                    t = bass.ds(v - 4, 1)
                    v_.tensor_tensor(x1[:, t, :].rearrange("p a d -> p (a d)"), psV[:, 0:D],
                                     x_res[:, t, :].rearrange("p a d -> p (a d)"), ALU.add).then_inc(out_done, 1)
                if runs(v0, 3, steady):
                    dve.wait_ge(rden_ready, v - 2)
                    for h2 in range(2):
                        r = slice(64 * h2, 64 * h2 + 64)
                        for b in range(2):
                            last = v_.tensor_tensor(att[s3][64 * b:64 * b + 64, :, h2, :],
                                                    pv[r, :, b, 8 * h2:8 * h2 + 8],
                                                    rden[s3][r, :, b:b + 1].to_broadcast([64, 8, 8]), ALU.mult)
                    last.then_inc(att_ready, 1)
                if runs(v0, 0, steady):
                    dve.wait_ge(qkv_sb, v + 1)
                    v_.tensor_copy(qk_hi[s][:], qk[s][:]).then_inc(hi_ready, 1)
                    dve.wait_ge(hi_ready, v + 1)
                    v_.tensor_tensor(qk_lo[s][:], qk[s][:], qk_hi[s][:], ALU.subtract)
                    for j in range(4):
                        last = v_.tensor_scalar(kbd[s][:, j, :], qk_hi[s][:, 1, :], mh[:, j:j + 1], None, ALU.mult)
                    last.then_inc(bd_ready, 1)
                if runs(v0, 1, steady):
                    largest(1)

            dve.wait_ge(pool_const, 1 + 5 * SLOTS)
            steps(dve, step)

        @block.scalar
        def _(act):
            a = nc.scalar
            a.dma_start(cst[:], consts).then_inc(c_in, 16)
            a.dma_start(bo_row[:], bo.to_broadcast([P, D])).then_inc(c_in, 16)
            act.wait_ge(pool_const, 1)
            a.activation(act_warm[:], half[:, 0:1], ACT.Exp)
            act.wait_ge(c_in, 32)
            act.wait_ge(const_ready, 11)
            act.wait_ge(pool_const, 1 + 5 * SLOTS)
            for i in range(4):
                act.wait_ge(wraw_in[i], 16)

            def step(v, v0, steady=False):
                s, s1, s2 = v0 % SLOTS, (v0 - 1) % SLOTS, (v0 - 2) % SLOTS
                first, last = runs(v0, 0, steady), runs(v0, 4, steady)
                if first or last:
                    act.wait_ge(colsT, v + 1)
                    c0, c1 = (0 if first else 1), (2 if last else 1)
                    a.copy(cols[s][:, c0:c1, :], psA[:, c0 * P:c1 * P]).then_inc(cols_sb, 1)
                if runs(v0, 2, steady):
                    act.wait_ge(mT_ps, v - 1)
                    a.copy(q_stack[s2][96:P], psR[0][96:P].rearrange("p g q -> p (g q)")[:, 0:256].bitcast(F16)
                           .rearrange("p (g q) -> p g q", g=4)).then_inc(mT_sb, 1)
                if runs(v0, 1, steady):
                    act.wait_ge(rep_ps, v)
                    a.copy(q_stack[s1][0:96], psR[0][0:96])
                    a.copy(k_stack[s1][0:96], psR[1][0:96]).then_inc(rep_sb, 1)
                if first:
                    act.wait_ge(qkv_ps, v + 1)
                    a.activation(qk[s][:, 1, :], psA[:, P:2 * P], ACT.Identity, bias=b_col[:, 1:2])
                    a.activation(qk[s][:, 0, :], psA[:, 0:P], ACT.Identity, bias=bq_s[:, 0:1], scale=SCALE)
                    for b in range(2):
                        r = slice(64 * b, 64 * b + 64)
                        ins = a.copy(vbd[s][r, b, :, 0:16],
                                     psA[r, 2 * P:3 * P].rearrange("p (h c) -> p h c", h=8))
                    ins.then_inc(qkv_sb, 1)
                if runs(v0, 2, steady):
                    act.wait_ge(t_ps, v - 1)
                    a.activation(pT[s2][:].rearrange("p g q -> p (g q)"), psT[:].rearrange("p a q -> p (a q)"),
                                 ACT.Exp).then_inc(exp_ready, 1)
                if runs(v0, 3, steady):
                    at = bass.ds(v - 3, 1)
                    a.copy(w_hi[:, at, :].rearrange("p a d -> p (a d)"),
                           w_raw[:, at, :].rearrange("p a d -> p (a d)")).then_inc(hi_split, 1)

            steps(act, step)

        @block.tensor
        def _(pe):
            t_ = nc.tensor
            pe.wait_ge(warm_ready, 1)
            for _ in range(WARM):
                t_.matmul(psS[:, 0, :], warm[:, 0:P], warm[:], start=True, stop=True)
            pe.wait_ge(w_in, 16)
            pe.wait_ge(const_ready, 11)
            t_.matmul(psV[:, 0:D], bv_mat[:], w[:, 3, :], start=True, stop=True).then_inc(bvo_ps, 1)

            def scores(v, v0, h):
                s1 = (v0 - 1) % SLOTS
                if h == 0:
                    pe.wait_ge(bd_ready, v)
                if v0 > 1 or h:
                    pe.wait_ge(max_ready, 2 * v - 2 + h)
                for gl in range(2):
                    g0 = 32 * (2 * h + gl)
                    for b in range(2):
                        c = slice(64 * b, 64 * b + 64)
                        last = t_.matmul(psS[c, gl, 0:256], qk_hi[s1][g0:g0 + 32, 0, c],
                                         kbd[s1][g0:g0 + 32, :, c], start=True, stop=True)
                last.then_inc(s_ps, 1)

            def step(v, v0, steady=False):
                s, s1, s2, s3, s4 = (v0 % SLOTS, (v0 - 1) % SLOTS, (v0 - 2) % SLOTS, (v0 - 3) % SLOTS,
                                     (v0 - 4) % SLOTS)
                if runs(v0, 0, steady) or runs(v0, 4, steady):
                    if v0 > 0 and runs(v0, 1, steady):
                        pe.wait_ge(qkv_sb, v)
                    if not runs(v0, 1, steady) and v0 > PAIRS:
                        pe.wait_ge(cols_sb, v)
                    if runs(v0, 0, steady):
                        pe.wait_ge(xh_ready, v + 1)
                        last = t_.transpose(psA[:, 0:P], xh[s][:], id32)
                    if runs(v0, 4, steady):
                        pe.wait_ge(att_ready, v - 3)
                        last = t_.transpose(psA[:, P:2 * P], att[s4][:].rearrange("p h b c -> p (h b c)"), id32)
                    last.then_inc(colsT, 1)
                if runs(v0, 2, steady):
                    pe.wait_ge(max_ready, 2 * v - 2)
                    if v0 > 2:
                        pe.wait_ge(mT_sb, v - 2)
                    mT = psR[0][96:P].rearrange("p g q -> p (g q)")[:, 0:256].bitcast(F16)
                    for g in range(4):
                        last = t_.transpose(mT[:, P * g:P * g + P], nmax[s2][:, g, :], id16[:])
                    last.then_inc(mT_ps, 1)
                if runs(v0, 1, steady):
                    scores(v, v0, 0)
                    if v0 > 1:
                        pe.wait_ge(rep_sb, v - 1)
                    for i in range(2):
                        for g in range(4):
                            t_.matmul(psR[i][0:96, g, :], sel[:, 2 * i, g, :], qk_hi[s1][:, i, :],
                                      start=True, stop=False)
                            last = t_.matmul(psR[i][0:96, g, :], sel[:, 2 * i + 1, g, :], qk_lo[s1][:, i, :],
                                             start=False, stop=True)
                    last.then_inc(rep_ps, 1)
                if runs(v0, 3, steady):
                    pe.wait_ge(exp_ready, v - 2)
                    if v0 > 3:
                        pe.wait_ge(att_ready, v - 3)
                    for hp in range(8):
                        last = t_.matmul(psV[:, P + 34 * hp:P + 34 * hp + 34],
                                         pT[s3][:, hp // 2, P * (hp % 2):P * (hp % 2) + P],
                                         vbd[s3][:, :, hp, :], start=True, stop=True)
                if runs(v0, 4, steady):
                    pe.wait_ge(cols_sb, v + 1)
                    last = t_.matmul(psV[:, 0:P], cols[s][:, 1, :], w[:, 3, :], start=True, stop=True)
                if runs(v0, 3, steady) or runs(v0, 4, steady):
                    last.then_inc(pv_ps, 1)
                if runs(v0, 0, steady):
                    pe.wait_ge(cols_sb, v + 1)
                    pe.wait_ge(ctx_in, 16 * v + 16)
                    t_.matmul(psA[:, 0:P], w[:, 0, :], cols[s][:, 0, :], start=True, stop=True)
                    t_.matmul(psA[:, P:2 * P], w[:, 1, :], ctx_sb[s][:], start=True, stop=True)
                    t_.matmul(psA[:, 2 * P:3 * P], ctx_sb[s][:], w[:, 2, :], start=True, stop=True).then_inc(qkv_ps, 1)
                if runs(v0, 1, steady):
                    scores(v, v0, 1)
                if runs(v0, 2, steady):
                    pe.wait_ge(qbd_ready, v - 1)
                    if v0 > 2:
                        pe.wait_ge(exp_ready, v - 2)
                    for g in range(4):
                        for b in range(2):
                            c = slice(64 * b, 64 * b + 64)
                            last = t_.matmul(psT[c, g // 2, 256 * (g % 2):256 * (g % 2) + 256],
                                             k_stack[s2][:, g, c], qbd[s2][:, g, :, c], start=True, stop=True)
                    last.then_inc(t_ps, 1)

            steps(pe, step)


def experts(nc, x1, w_hi, w_lo, rows, cols, b1, b2, out):
    with ExitStack() as stack:
        def sb(name, shape, dt=F32):
            return stack.enter_context(nc.sbuf_tensor(name, shape, dt))

        def pb(name, shape, dt=F32):
            return stack.enter_context(nc.psum_tensor(name, shape, dt))

        def sem(name):
            return stack.enter_context(nc.semaphore(name))

        row_sb = sb("row_sb", [P, 2 * D + 2 * EXPERTS])
        ln_w, ln_b = row_sb[:, 0:D], row_sb[:, D:2 * D]
        r_b, iota = row_sb[:, 2 * D:2 * D + EXPERTS], row_sb[:, 2 * D + EXPERTS:]
        col_sb = sb("col_sb", [P, P + EXPERTS])
        id32, r_w = col_sb[:, 0:P], col_sb[:, P:]
        b1_sb = sb("b1_sb", [P, EXPERTS, FC])
        b1_now = sb("b1_now", [P, FC])
        b2_sb = sb("b2_sb", [EXPERTS, D])
        half = sb("f_half", [P, PAIRS])
        mraw = sb("mraw", [P, PAIRS, 6])
        mv = sb("f_mv", [P, PAIRS, 2])
        veps = sb("f_veps", [P, PAIRS])
        rstd = sb("f_rstd", [P, PAIRS])
        oraw = sb("oraw", [P, PAIRS, 6])
        omv = sb("omv", [P, PAIRS, 2])
        oveps = sb("oveps", [P, PAIRS])
        orstd = sb("orstd", [P, PAIRS])
        acc = sb("acc", [P, PAIRS, D])
        xT = sb("xT", [P, TOKENS])
        xT_hi = sb("xT_hi", [P, TOKENS], F16)
        xT_lo = sb("xT_lo", [P, TOKENS], F16)
        logits = sb("logits", [P, PAIRS, EXPERTS])
        top = sb("top", [P, PAIRS, 8])
        top_i = sb("top_i", [P, PAIRS, 8], mybir.dt.uint32)
        top_f = sb("top_f", [P, PAIRS, 2])
        gap = sb("gap", [P, PAIRS])
        ratio = sb("ratio", [P, PAIRS])
        denom = sb("denom", [P, PAIRS])
        wt = sb("wt", [P, PAIRS, 2])
        one_hot = [sb(f"one_hot{i}", [P, PAIRS, EXPERTS]) for i in range(2)]
        cw = sb("cw", [P, PAIRS, EXPERTS])
        cwT = sb("cwT", [EXPERTS, TOKENS])
        h = [sb(f"h{i}", [P, FC, 512]) for i in range(2)]
        h_hi = [sb(f"h_hi{i}", [P, FC, 512], F16) for i in range(2)]
        h_lo = [sb(f"h_lo{i}", [P, FC, 512], F16) for i in range(2)]
        res = sb("res", [P, BT, D])

        psH = pb("psH", [P, FC, 512])
        psY = pb("psY", [P, 2, BT, D])
        psL = pb("psL", [P, PAIRS, EXPERTS])
        psC = pb("psC", [EXPERTS, 4 * P])

        row_in = sem("row_in")
        col_in = sem("col_in")
        bias_in = sem("bias_in")
        bias_set = sem("bias_set")
        half_set = sem("half_set")
        raw_done = sem("raw_done")
        mv_ready = sem("mv_ready")
        veps_ready = sem("veps_ready")
        rstd_ready = sem("f_rstd_ready")
        x2_ready = sem("x2_ready")
        x2T_ps = sem("x2T_ps")
        xT_ready = sem("xT_ready")
        xhi_ready = sem("xhi_ready")
        xlo_ready = sem("xlo_ready")
        logits_ps = sem("logits_ps")
        route = sem("route")
        gap_ready = sem("gap_ready")
        ratio_ready = sem("ratio_ready")
        cw_ready = sem("cw_ready")
        cwT_ps = sem("cwT_ps")
        cwT_ready = sem("cwT_ready")
        b2_ps = sem("b2_ps")
        b2_used = sem("b2_used")
        h_ps = sem("h_ps")
        gelu_ready = sem("gelu_ready")
        hhi_ready = sem("hhi_ready")
        split_ready = sem("split_ready")
        y_ps = sem("y_ps")
        y_added = sem("y_added")
        oraw_done = sem("oraw_done")
        omv_ready = sem("omv_ready")
        oveps_ready = sem("oveps_ready")
        orstd_ready = sem("orstd_ready")
        fin_done = sem("fin_done")
        x1b_ready = sem("x1b_ready")
        y_out = sem("y_out")
        stored = sem("stored")

        def tile(a, t):
            return a[:, t, :]

        block = stack.enter_context(nc.Block())

        @block.sync
        def _(sp):
            sp.dma_start(col_sb[:], cols).then_inc(col_in, 16)
            sp.dma_start(row_sb[:], rows.to_broadcast([P, 2 * D + 2 * EXPERTS])).then_inc(row_in, 16)
            sp.dma_start(b1_sb[:], b1).then_inc(bias_in, 16)
            sp.dma_start(b2_sb[:], b2).then_inc(bias_in, 16)
            out_t = out.rearrange("(t p) d -> p t d", p=P)
            for k in range(BLOCKS):
                sp.wait_ge(y_out, BT * (k + 1))
                sp.dma_start(out_t[:, BT * k:BT * k + BT, :], x1[:, BT * k:BT * k + BT, :]).then_inc(stored, 16)
            sp.wait_ge(stored, 16 * BLOCKS)

        @block.gpsimd
        def _(pool):
            g = nc.gpsimd
            g.memset(half[:], -0.5).then_inc(half_set, 1)
            for k in range(BLOCKS):
                t = slice(BT * k, BT * k + BT)
                pool.wait_ge(mv_ready, BT * (k + 1))
                g.tensor_scalar(veps[:, t], mv[:, t, 1], EPS_IN, 1.0, ALU.add, ALU.mult).then_inc(veps_ready, 1)
                pool.wait_ge(half_set, 1)
                pool.wait_ge(veps_ready, k + 1)
                g.tensor_tensor(rstd[:, t], veps[:, t], half[:, t], ALU.pow).then_inc(rstd_ready, 1)
            pool.wait_ge(row_in, 16)
            pool.wait_ge(x2_ready, PAIRS)
            for t in range(PAIRS):
                g.tensor_tensor(tile(x1, t), tile(x1, t), ln_b, ALU.add).then_inc(x1b_ready, 1)
            for k in range(BLOCKS):
                t = slice(BT * k, BT * k + BT)
                pool.wait_ge(omv_ready, BT * (k + 1))
                g.tensor_scalar(oveps[:, t], omv[:, t, 1], EPS_OUT, 1.0, ALU.add, ALU.mult).then_inc(oveps_ready, 1)
                pool.wait_ge(oveps_ready, k + 1)
                g.tensor_tensor(orstd[:, t], oveps[:, t], half[:, t], ALU.pow).then_inc(orstd_ready, 1)

        @block.vector
        def _(dve):
            v = nc.vector

            def split_x(k):
                dve.wait_ge(xT_ready, k + 1)
                c = slice(512 * k, 512 * k + 512)
                v.tensor_copy(xT_hi[:, c], xT[:, c]).then_inc(xhi_ready, 1)
                dve.wait_ge(xhi_ready, k + 1)
                v.tensor_tensor(xT_lo[:, c], xT[:, c], xT_hi[:, c], ALU.subtract).then_inc(xlo_ready, 1)

            for t in range(PAIRS):
                v.bn_stats(mraw[:, t, :], tile(x1, t)).then_inc(raw_done, 1)
            for t in range(PAIRS):
                dve.wait_ge(raw_done, t + 1)
                v.bn_aggr(mv[:, t, :], mraw[:, t, :]).then_inc(mv_ready, 1)
            for k in range(BLOCKS):
                dve.wait_ge(rstd_ready, k + 1)
                for t in range(BT * k, BT * k + BT):
                    v.tensor_scalar(tile(acc, t), tile(x1, t), mv[:, t, 0:1], rstd[:, t:t + 1],
                                    ALU.subtract, ALU.mult).then_inc(x2_ready, 1)
                if k:
                    split_x(k - 1)
            split_x(BLOCKS - 1)
            dve.wait_ge(row_in, 16)
            dve.wait_ge(logits_ps, BLOCKS)
            v.tensor_tensor(logits[:], psL[:], r_b.unsqueeze(1).to_broadcast([P, PAIRS, EXPERTS]),
                            ALU.add).then_inc(route, 1)
            dve.wait_ge(route, 1)
            for t in range(PAIRS):
                v.max(top[:, t, :], logits[:, t, :]).then_inc(route, 1)
            for t in range(PAIRS):
                dve.wait_ge(route, 2 + t)
                v.max_index(top_i[:, t, :], top[:, t, :], logits[:, t, :]).then_inc(route, 1)
            n = 1 + 2 * PAIRS
            v.tensor_tensor(gap[:], top[:, :, 1], top[:, :, 0], ALU.subtract).then_inc(gap_ready, 1)
            dve.wait_ge(route, n)
            v.tensor_copy(top_f[:], top_i[:, :, 0:2]).then_inc(route, 1)
            dve.wait_ge(route, n + 1)
            for i in range(2):
                v.tensor_tensor(one_hot[i][:], top_f[:, :, i:i + 1].to_broadcast([P, PAIRS, EXPERTS]),
                                iota.unsqueeze(1).to_broadcast([P, PAIRS, EXPERTS]), ALU.is_equal).then_inc(route, 1)
            dve.wait_ge(ratio_ready, 1)
            v.tensor_scalar(denom[:], ratio[:], 1.0, None, ALU.add).then_inc(route, 1)
            dve.wait_ge(route, n + 4)
            v.reciprocal(wt[:, :, 0], denom[:]).then_inc(route, 1)
            dve.wait_ge(route, n + 5)
            v.tensor_tensor(wt[:, :, 1], wt[:, :, 0], ratio[:], ALU.mult).then_inc(route, 1)
            dve.wait_ge(route, n + 6)
            for i in range(2):
                v.tensor_tensor(one_hot[i][:], one_hot[i][:], wt[:, :, i:i + 1].to_broadcast([P, PAIRS, EXPERTS]),
                                ALU.mult).then_inc(route, 1)
            dve.wait_ge(route, n + 8)
            v.tensor_tensor(cw[:], one_hot[0][:], one_hot[1][:], ALU.add).then_inc(cw_ready, 1)
            for k in range(BLOCKS):
                dve.wait_ge(b2_ps, k + 1)
                v.tensor_tensor(acc[:, BT * k:BT * k + BT, :], acc[:, BT * k:BT * k + BT, :], psY[:, k % 2],
                                ALU.add).then_inc(b2_used, 1)

            def split(item, k):
                for c in range(FC):
                    dve.wait_ge(gelu_ready, item * FC + (c + 1))
                    if k > 1 or not isinstance(item, int) or item > 1:
                        if c == 0:
                            dve.wait_ge(y_ps, item - 1)
                    v.tensor_copy(h_hi[k % 2][:, c, :], h[k % 2][:, c, :]).then_inc(hhi_ready, 1)
                    dve.wait_ge(hhi_ready, item * FC + (c + 1))
                    v.tensor_tensor(h_lo[k % 2][:, c, :], h[k % 2][:, c, :], h_hi[k % 2][:, c, :],
                                    ALU.subtract).then_inc(split_ready, 1)

            def add(item, e, k):
                dve.wait_ge(y_ps, item + 1)
                for t in range(BT * k, BT * k + BT):
                    last = v.scalar_tensor_tensor(tile(acc, t), psY[:, k % 2, t % BT, :],
                                                  cw[:, t, bass.ds(e, 1)], tile(acc, t), ALU.mult, ALU.add)
                last.then_inc(y_added, 1)

            for k in range(BLOCKS):
                split(k, k)
                if k:
                    add(k - 1, 0, k - 1)
                else:
                    dve.wait_ge(b2_used, BLOCKS)
            with dve.Fori(1, EXPERTS) as e:
                for k in range(BLOCKS):
                    split(e * BLOCKS + k, k + 2)
                    dve.wait_ge(y_added, e * BLOCKS + (k - 1))
                    add(e * BLOCKS + (k - 1), e - 1 if k == 0 else e, (k - 1) % BLOCKS)
            add(EXPERTS * BLOCKS - 1, EXPERTS - 1, BLOCKS - 1)
            dve.wait_ge(y_added, EXPERTS * BLOCKS)
            for t in range(PAIRS):
                v.bn_stats(oraw[:, t, :], tile(acc, t)).then_inc(oraw_done, 1)
            for t in range(PAIRS):
                dve.wait_ge(oraw_done, t + 1)
                v.bn_aggr(omv[:, t, :], oraw[:, t, :]).then_inc(omv_ready, 1)
            dve.wait_ge(x1b_ready, PAIRS)
            m = 0
            for k in range(BLOCKS):
                dve.wait_ge(orstd_ready, k + 1)
                for t in range(BT * k, BT * k + BT):
                    v.tensor_scalar(tile(acc, t), tile(acc, t), omv[:, t, 0:1], orstd[:, t:t + 1],
                                    ALU.subtract, ALU.mult).then_inc(fin_done, 1)
                for t in range(BT * k, BT * k + BT):
                    dve.wait_ge(fin_done, 2 * BT * k + t % BT + 1)
                    v.tensor_tensor(tile(acc, t), tile(acc, t), ln_w, ALU.mult).then_inc(fin_done, 1)
                for t in range(BT * k, BT * k + BT):
                    dve.wait_ge(fin_done, 2 * BT * k + BT + t % BT + 1)
                    v.tensor_tensor(tile(x1, t), tile(x1, t), tile(acc, t), ALU.add).then_inc(y_out, 1)

        @block.scalar
        def _(act):
            a = nc.scalar
            for k in range(BLOCKS):
                act.wait_ge(x2T_ps, k + 1)
                a.copy(xT[:, 512 * k:512 * k + 512], psH[:, k, :]).then_inc(xT_ready, 1)
            act.wait_ge(gap_ready, 1)
            a.activation(ratio[:], gap[:], ACT.Exp).then_inc(ratio_ready, 1)
            for k in range(BLOCKS):
                act.wait_ge(cwT_ps, k + 1)
                a.copy(cwT[:, 512 * k:512 * k + 512], psC[:]).then_inc(cwT_ready, 1)
            act.wait_ge(bias_in, 32)

            def gelu(item, e, k, reused):
                if k == 0:
                    if not isinstance(e, int):
                        act.wait_ge(gelu_ready, item * FC)
                    a.copy(b1_now[:], b1_sb[:, bass.ds(e, 1), :].rearrange("p a c -> p (a c)")).then_inc(bias_set, 1)
                    act.wait_ge(bias_set, e + 1)
                for c in range(FC):
                    act.wait_ge(h_ps, item * FC + (c + 1))
                    if reused:
                        act.wait_ge(split_ready, (item - 2) * FC + (c + 1))
                    a.activation(h[k % 2][:, c, :], psH[:, c, :], ACT.Gelu,
                                 bias=b1_now[:, c:c + 1]).then_inc(gelu_ready, 1)

            for k in range(BLOCKS):
                gelu(k, 0, k, k >= 2)
            with act.Fori(1, EXPERTS) as e:
                for k in range(BLOCKS):
                    gelu(e * BLOCKS + k, e, k, True)

        @block.tensor
        def _(pe):
            t_ = nc.tensor
            pe.wait_ge(col_in, 16)
            for k in range(BLOCKS + 1):
                if k < BLOCKS:
                    for t in range(BT * k, BT * k + BT):
                        pe.wait_ge(x2_ready, t + 1)
                        last = t_.transpose(psH[:, k, P * (t % BT):P * (t % BT) + P], tile(acc, t), id32)
                    last.then_inc(x2T_ps, 1)
                if k > 0:
                    pe.wait_ge(xT_ready, k)
                    for t in range(BT * k - BT, BT * k):
                        last = t_.matmul(psL[:, t, :], xT[:, P * t:P * t + P], r_w, start=True, stop=True)
                    last.then_inc(logits_ps, 1)
            pe.wait_ge(cw_ready, 1)
            pe.wait_ge(bias_in, 32)
            for k in range(BLOCKS):
                if k:
                    pe.wait_ge(cwT_ready, k)
                for t in range(BT * k, BT * k + BT):
                    last = t_.transpose(psC[:, P * (t % BT):P * (t % BT) + P], cw[:, t, :], id32)
                last.then_inc(cwT_ps, 1)
                pe.wait_ge(cwT_ready, k + 1)
                if k >= 2:
                    pe.wait_ge(b2_used, k - 1)
                for t in range(BT * k, BT * k + BT):
                    last = t_.matmul(psY[:, k % 2, t % BT, :], cwT[:, P * t:P * t + P], b2_sb[:], start=True, stop=True)
                last.then_inc(b2_ps, 1)

            def hidden(item, e, k, first):
                tok = slice(512 * k, 512 * k + 512)
                for c in range(FC):
                    if not first:
                        pe.wait_ge(gelu_ready, (item - 1) * FC + (c + 1))
                    w1_hi = w_hi[:, bass.ds(2 * e, 1), P * c:P * c + P].rearrange("p a f -> p (a f)")
                    w1_lo = w_lo[:, bass.ds(2 * e, 1), P * c:P * c + P].rearrange("p a f -> p (a f)")
                    t_.matmul(psH[:, c, :], w1_hi, xT_hi[:, tok], start=True, stop=False)
                    t_.matmul(psH[:, c, :], w1_hi, xT_lo[:, tok], start=False, stop=False)
                    t_.matmul(psH[:, c, :], w1_lo, xT_hi[:, tok], start=False, stop=True).then_inc(h_ps, 1)

            def output(item, e, k, reused):
                if reused:
                    pe.wait_ge(y_added, item - 1)
                for t in range(BT):
                    r = slice(P * t, P * t + P)
                    for c in range(FC):
                        if t == 0:
                            pe.wait_ge(split_ready, item * FC + (c + 1))
                        w2_hi = w_hi[:, bass.ds(2 * e + 1, 1), P * c:P * c + P].rearrange("p a f -> p (a f)")
                        w2_lo = w_lo[:, bass.ds(2 * e + 1, 1), P * c:P * c + P].rearrange("p a f -> p (a f)")
                        y = psY[:, k % 2, t, :]
                        t_.matmul(y, h_hi[k % 2][:, c, r], w2_hi, start=c == 0, stop=False)
                        t_.matmul(y, h_hi[k % 2][:, c, r], w2_lo, start=False, stop=False)
                        last = t_.matmul(y, h_lo[k % 2][:, c, r], w2_hi, start=False, stop=c == FC - 1)
                last.then_inc(y_ps, 1)

            pe.wait_ge(xlo_ready, BLOCKS)
            for k in range(BLOCKS):
                hidden(k, 0, k, k == 0)
                if k == 1:
                    pe.wait_ge(b2_used, BLOCKS)
                if k:
                    output(k - 1, 0, k - 1, k > 2)
            with pe.Fori(1, EXPERTS) as e:
                for k in range(BLOCKS):
                    hidden(e * BLOCKS + k, e, k, False)
                    output(e * BLOCKS + (k - 1), e - 1 if k == 0 else e, (k - 1) % BLOCKS, True)
            output(EXPERTS * BLOCKS - 1, EXPERTS - 1, BLOCKS - 1, True)


def xattn_moe_kernel(nc, x, ctxT, w4, consts, bo, w_ffn, rows, cols, b1, b2, out):
    with ExitStack() as stack:
        x1 = stack.enter_context(nc.sbuf_tensor("x1", [P, PAIRS, D], F32))
        w_hi = stack.enter_context(nc.sbuf_tensor("w_hi", [P, 2 * EXPERTS, 512], F16))
        w_lo = stack.enter_context(nc.sbuf_tensor("w_lo", [P, 2 * EXPERTS, 512], F16))
        attention(nc, x1, w_hi, w_lo, x, ctxT, w4, consts, bo, w_ffn)
        experts(nc, x1, w_hi, w_lo, rows, cols, b1, b2, out)


def kernel(**inputs):
    import numpy as np
    import concourse.bacc as bacc
    from concourse.bass_utils import run_bass_kernel_spmd

    d = {name: np.asarray(a) for name, a in inputs.items()}
    att = {name: d["L0_xattn_" + name] for name in ("Wq", "Wk", "Wv", "Wo", "bq", "bk", "bv", "bo")}
    ffn = {name: d["L0_ffn_" + name] for name in
           ("router_w", "router_b", "w1", "b1", "w2", "b2", "ln_w", "ln_b")}
    p = np.arange(P)
    eye = np.eye(P, dtype=np.float32)
    own_group = ((p[:, None] // HD) % 4 == np.arange(4)).astype(np.float32)
    own_row = (np.where(p[:, None] < 96, (p[:, None] // HD) % 4, p[:, None] - 96) == np.arange(4)).astype(np.float32)
    w1 = ffn["w1"].transpose(2, 0, 1)
    w2 = ffn["w2"].transpose(2, 0, 1).reshape(FC, P, EXPERTS, D).transpose(1, 2, 0, 3).reshape(P, EXPERTS, FF)
    arrays = {
        "x_rows": d["x"].reshape(TOKENS, D),
        "ctxT": d["ctx_1024"].reshape(TOKENS, D).T,
        "w4": np.stack([att[name].T for name in ("Wq", "Wk", "Wv", "Wo")], 1),
        "consts": np.concatenate([eye, own_group, own_row] + [att[b].reshape(D, 1) for b in ("bq", "bk", "bv")], 1),
        "bo": att["bo"].reshape(1, D),
        "w_ffn": np.stack([w1, w2], 2).reshape(P, 2 * EXPERTS, FF),
        "rows": np.concatenate([ffn["ln_w"], ffn["ln_b"], ffn["router_b"],
                                np.arange(EXPERTS, dtype=np.float32)]).reshape(1, -1),
        "cols": np.concatenate([eye, ffn["router_w"].T], 1),
        "b1": ffn["b1"].reshape(EXPERTS, FC, P).transpose(2, 0, 1),
        "b2": ffn["b2"],
    }
    arrays = {name: np.ascontiguousarray(a) for name, a in arrays.items()}
    nc = bacc.Bacc("TRN2", target_bir_lowering=False, num_devices=1)
    args = [nc.dram_tensor(name, a.shape, mybir.dt.from_np(a.dtype), kind="ExternalInput").ap()
            for name, a in arrays.items()]
    out = nc.dram_tensor("out", (TOKENS, D), F32, kind="ExternalOutput").ap()
    xattn_moe_kernel(nc, *args, out)
    r = run_bass_kernel_spmd(nc, [arrays], core_ids=[0])
    return r.results[0]["out"].reshape(BATCH, SEQ, D)
```

```python
from contextlib import ExitStack

import concourse.bass as bass
from concourse import mybir

ALU = mybir.AluOpType
ACT = mybir.ActivationFunctionType
AX = mybir.AxisListType
F32 = mybir.dt.float32
F16 = mybir.dt.float16
BF16 = mybir.dt.bfloat16

P = 128
D = 128
HEADS = 16
HD = D // HEADS
BATCH, SEQ = 32, 64
TOKENS = BATCH * SEQ
PAIRS = TOKENS // P
SLOTS = 3
STAGES = 4
EXPERTS = 8
FF = 512
FC = FF // P
BLOCKS = TOKENS // 512
BT = 512 // P
EPS_OUT = 1e-12
SLOT_TILES = (2 * TOKENS) // P + EXPERTS - 1
ROW_AT = [0]
for width in (D, D, EXPERTS, EXPERTS * EXPERTS, PAIRS, P, EXPERTS * D):
    ROW_AT.append(ROW_AT[-1] + width)
ROW_WIDTH = ROW_AT[-1]
WARM = 10
CHUNK = 4
SCALE = float(HD) ** -0.5
EPS_IN = 1e-5


def attention(nc, x1, w_hi, w_lo, x, ctxT, w4, consts, bo, w_ffn):
    with ExitStack() as stack:
        def sb(name, shape, dt=F32):
            return stack.enter_context(nc.sbuf_tensor(name, shape, dt))

        def pb(name, shape, dt=F32):
            return stack.enter_context(nc.psum_tensor(name, shape, dt))

        def sem(name):
            return stack.enter_context(nc.semaphore(name))

        x_sb = sb("x_sb", [P, PAIRS, D])
        x_res = sb("x_res", [P, PAIRS, D])
        w_raw = sb("w_raw", [P, 2 * EXPERTS, 512])
        ctx_sb = [sb(f"ctx{i}", [P, P]) for i in range(SLOTS)]
        w = sb("w", [P, 4, D])
        cst = sb("cst", [P, P + 11])
        id32, mh, mm, b_col = cst[:, 0:P], cst[:, P:P + 4], cst[:, P + 4:P + 8], cst[:, P + 8:P + 11]
        bq_s = sb("bq_s", [P, 1])
        bo_row = sb("bo_row", [P, D])
        bv_mat = sb("bv_mat", [P, P])
        bvo = sb("bvo", [P, D])
        id16 = sb("id16", [P, P], F16)
        sel = sb("sel", [P, 4, 4, 96], F16)
        stats = sb("stats", [P, PAIRS, 6])
        mv = sb("mv", [P, PAIRS, 2])
        half = sb("half", [P, PAIRS])
        veps = sb("veps", [P, PAIRS])
        rstd = sb("rstd", [P, PAIRS])
        nmr = sb("nmr", [P, PAIRS])
        nmean = sb("nmean", [P, PAIRS])
        xh = [sb(f"xh{i}", [P, D]) for i in range(SLOTS)]
        xr = [sb(f"xr{i}", [P, D]) for i in range(SLOTS)]
        cols = [sb(f"cols{i}", [P, 2, P]) for i in range(SLOTS)]
        qk = [sb(f"qk{i}", [P, 2, P]) for i in range(SLOTS)]
        qk_hi = [sb(f"qk_hi{i}", [P, 2, P], F16) for i in range(SLOTS)]
        qk_lo = [sb(f"qk_lo{i}", [P, 2, P], F16) for i in range(SLOTS)]
        kbd = [sb(f"kbd{i}", [P, 4, P], F16) for i in range(SLOTS)]
        q_stack = [sb(f"q_stack{i}", [P, 4, P], F16) for i in range(SLOTS)]
        k_stack = [sb(f"k_stack{i}", [P, 4, P], F16) for i in range(SLOTS)]
        qbd = [sb(f"qbd{i}", [P, 4, 4, P], F16) for i in range(SLOTS)]
        vbd = [sb(f"vbd{i}", [P, 2, 8, 17]) for i in range(SLOTS)]
        nmax = [sb(f"nmax{i}", [P, 4, 32], F16) for i in range(SLOTS)]
        pT = [sb(f"pT{i}", [P, 4, 256]) for i in range(SLOTS)]
        rden = [sb(f"rden{i}", [P, 8, 2]) for i in range(SLOTS)]
        att = [sb(f"att{i}", [P, 8, 2, HD]) for i in range(SLOTS)]

        psS = pb("psS", [P, 2, 512])
        psT = pb("psT", [P, 2, 512])
        psR = [pb("psRq", [P, 4, P]), pb("psRk", [P, 4, P])]
        psA = pb("psA", [P, 512])
        psV = pb("psV", [P, 512])

        act_warm = sb("act_warm", [P, 1])
        warm = sb("warm", [P, 512], BF16)
        warm_ready = sem("warm_ready")
        x_in = [sem(f"x_in{c}") for c in range(PAIRS // CHUNK)]
        wraw_in = [sem(f"wraw_in{i}") for i in range(4)]
        hi_split = sem("hi_split")
        lo_split = sem("lo_split")
        ctx_in = sem("ctx_in")
        w_in = sem("w_in")
        c_in = sem("c_in")
        const_ready = sem("const_ready")
        pool_const = sem("pool_const")
        stats_raw = sem("stats_raw")
        stats_ready = sem("stats_ready")
        rs = sem("rs")
        bvo_ps = sem("bvo_ps")
        bvo_sb = sem("bvo_sb")
        res_ready = sem("res_ready")
        xh_ready = sem("xh_ready")
        xr_ready = sem("xr_ready")
        xT_ps = sem("xT_ps")
        xT_sb = sem("xT_sb")
        attT_ps = sem("attT_ps")
        attT_sb = sem("attT_sb")
        lo_ready = sem("lo_ready")
        qkv_ps = sem("qkv_ps")
        qk_sb = sem("qk_sb")
        v_sb = sem("v_sb")
        bd_ready = sem("bd_ready")
        s_ps = sem("s_ps")
        max_ready = sem("max_ready")
        mT_ps = sem("mT_ps")
        rep_ps = sem("rep_ps")
        rep_sb = sem("rep_sb")
        mT_sb = sem("mT_sb")
        qbd_ready = sem("qbd_ready")
        hi_ready = sem("hi_ready")
        t_ps = sem("t_ps")
        exp_ready = sem("exp_ready")
        pv_ps = sem("pv_ps")
        rden_ready = sem("rden_ready")
        att_ready = sem("att_ready")
        out_done = sem("out_done")

        x_t = x.rearrange("(t p) d -> p t d", p=P)

        block = stack.enter_context(nc.Block())

        def steps(engine, step):
            for v in range(STAGES):
                step(v, v)
            with engine.Fori(0, (PAIRS - STAGES) // SLOTS) as i:
                for k in range(SLOTS):
                    step(i * SLOTS + (STAGES + k), STAGES + k, True)
            for v in range(PAIRS, PAIRS + STAGES):
                step(v, v)

        def runs(v0, lag, steady):
            return steady or 0 <= v0 - lag < PAIRS

        @block.sync
        def _(sp):
            sp.dma_start(x_sb[:, 0:CHUNK, :], x_t[:, 0:CHUNK, :]).then_inc(x_in[0], 16)
            sp.dma_start(w[:], w4).then_inc(w_in, 16)
            sp.dma_start(ctx_sb[0][:], ctxT[:, 0:P]).then_inc(ctx_in, 16)
            for c in range(1, PAIRS // CHUNK):
                sp.dma_start(x_sb[:, c * CHUNK:(c + 1) * CHUNK, :],
                             x_t[:, c * CHUNK:(c + 1) * CHUNK, :]).then_inc(x_in[c], 16)
            for v in range(1, PAIRS):
                sp.wait_ge(ctx_in, 16 * v)
                if v >= SLOTS:
                    sp.wait_ge(qkv_ps, v - SLOTS + 1)
                sp.dma_start(ctx_sb[v % SLOTS][:], ctxT[:, v * P:(v + 1) * P]).then_inc(ctx_in, 16)
                if v == 2:
                    for i in range(4):
                        sp.dma_start(w_raw[:, 4 * i:4 * i + 4, :], w_ffn[:, 4 * i:4 * i + 4, :]).then_inc(wraw_in[i], 16)

        @block.gpsimd
        def _(pool):
            g = nc.gpsimd
            g.memset(half[:], -0.5).then_inc(pool_const, 1)
            for i in range(SLOTS):
                g.memset(vbd[i][:], 0.0).then_inc(pool_const, 1)
                g.memset(nmax[i][:], 0.0).then_inc(pool_const, 1)
            pool.wait_ge(pool_const, 1 + 2 * SLOTS)
            for i in range(SLOTS):
                g.memset(k_stack[i][96:P], 1.0).then_inc(pool_const, 1)
            pool.wait_ge(pool_const, 1 + 3 * SLOTS)
            for i in range(SLOTS):
                for b in range(2):
                    g.memset(vbd[i][64 * b:64 * b + 64, b, :, 16:17], 1.0).then_inc(pool_const, 1)
            pool.wait_ge(pool_const, 1 + 5 * SLOTS)
            def rstd_of(c):
                t = slice(c * CHUNK, (c + 1) * CHUNK)
                pool.wait_ge(stats_ready, (c + 1) * CHUNK)
                g.tensor_scalar(veps[:, t], mv[:, t, 1], EPS_IN, 1.0, ALU.add, ALU.mult).then_inc(rs, 1)
                g.tensor_scalar(nmean[:, t], mv[:, t, 0], -1.0, 1.0, ALU.mult, ALU.mult).then_inc(rs, 1)
                pool.wait_ge(rs, 4 * c + 2)
                g.tensor_tensor(rstd[:, t], veps[:, t], half[:, t], ALU.pow).then_inc(rs, 1)
                pool.wait_ge(rs, 4 * c + 3)
                g.tensor_tensor(nmr[:, t], nmean[:, t], rstd[:, t], ALU.mult).then_inc(rs, 1)
                pool.wait_ge(rs, 4 * c + 4)

            def normalise(v, s, reused):
                at = bass.ds(v, 1)
                g.tensor_tensor(xr[s][:], x_sb[:, at, :].rearrange("p a d -> p (a d)"),
                                rstd[:, at].to_broadcast([P, D]), ALU.mult).then_inc(xr_ready, 1)
                if reused:
                    pool.wait_ge(xT_ps, v - (SLOTS - 1))
                    pool.nop()
                pool.wait_ge(xr_ready, v + 1)
                pool.nop()
                g.tensor_tensor(xh[s][:], xr[s][:], nmr[:, at].to_broadcast([P, D]), ALU.add).then_inc(xh_ready, 1)

            def residual(v):
                at = bass.ds(v, 1)
                g.tensor_tensor(x_res[:, at, :].rearrange("p a d -> p (a d)"),
                                x_sb[:, at, :].rearrange("p a d -> p (a d)"), bvo[:], ALU.add).then_inc(res_ready, 1)

            def low_part(v):
                at = bass.ds(v, 1)
                pool.wait_ge(hi_split, v + 1)
                pool.nop()
                g.tensor_tensor(w_lo[:, at, :].rearrange("p a d -> p (a d)"),
                                w_raw[:, at, :].rearrange("p a d -> p (a d)"),
                                w_hi[:, at, :].rearrange("p a d -> p (a d)"), ALU.subtract).then_inc(lo_split, 1)

            rstd_of(0)
            for v in range(SLOTS):
                normalise(v, v, False)
            for c in range(1, PAIRS // CHUNK):
                rstd_of(c)
            normalise(SLOTS, 0, True)
            pool.wait_ge(bvo_sb, 1)
            with pool.Fori(0, (PAIRS - STAGES) // SLOTS) as i:
                for k in range(SLOTS):
                    residual(i * SLOTS + k)
                    normalise(i * SLOTS + (STAGES + k), (STAGES + k) % SLOTS, True)
                    low_part(i * SLOTS + k)
            for v in range(PAIRS - STAGES, PAIRS):
                residual(v)
                low_part(v)

        @block.vector
        def _(dve):
            v_ = nc.vector
            v_.memset(warm[:], 0.0).then_inc(warm_ready, 1)

            def chunk_stats(c):
                dve.wait_ge(x_in[c], 16)
                for t in range(c * CHUNK, (c + 1) * CHUNK):
                    v_.bn_stats(stats[:, t, :], x_sb[:, t, :]).then_inc(stats_raw, 1)
                for t in range(c * CHUNK, (c + 1) * CHUNK):
                    dve.wait_ge(stats_raw, t + 1)
                    v_.bn_aggr(mv[:, t, :], stats[:, t, :]).then_inc(stats_ready, 1)

            chunk_stats(0)
            dve.wait_ge(c_in, 32)
            v_.tensor_copy(id16[:], id32).then_inc(const_ready, 1)
            v_.memset(sel[:], 0.0).then_inc(const_ready, 1)
            v_.memset(bv_mat[:], 1.0).then_inc(const_ready, 1)
            v_.tensor_scalar(bq_s[:], b_col[:, 0:1], SCALE, None, ALU.mult).then_inc(const_ready, 1)
            dve.wait_ge(const_ready, 4)
            for i, blocks in enumerate(((0, 2), (1,), (0, 1), (2,))):
                for k in blocks:
                    v_.tensor_copy(sel[:, i, :, 32 * k:32 * k + 32],
                                   id16[:].rearrange("p (g c) -> p g c", g=4)).then_inc(const_ready, 1)
            v_.tensor_scalar(bv_mat[:], bv_mat[:], b_col[:, 2:3], None, ALU.mult).then_inc(const_ready, 1)
            dve.wait_ge(bvo_ps, 1)
            v_.tensor_tensor(bvo[:], psV[:, 0:D], bo_row[:], ALU.add).then_inc(bvo_sb, 1)
            for c in range(1, PAIRS // CHUNK):
                chunk_stats(c)

            def step(v, v0, steady=False):
                s = v0 % SLOTS
                s2, s3 = (v0 - 2) % SLOTS, (v0 - 3) % SLOTS

                def largest(lag, h):
                    dve.wait_ge(s_ps, 2 * v + (1 + h - 2 * lag))
                    v_.tensor_reduce(nmax[(v0 - lag) % SLOTS][:, 2 * h:2 * h + 2, 0:4],
                                     psS[:, :, 0:256].rearrange("p g (h k) -> p g h k", h=4),
                                     AX.X, ALU.max, negate=True).then_inc(max_ready, 1)

                if runs(v0, 2, steady):
                    largest(2, 1)
                if runs(v0, 1, steady):
                    largest(1, 0)
                if runs(v0, 0, steady):
                    dve.wait_ge(qk_sb, v + 1)
                    v_.tensor_copy(qk_hi[s][:], qk[s][:]).then_inc(hi_ready, 1)
                if runs(v0, 2, steady):
                    dve.wait_ge(mT_sb, v - 1)
                    for j in range(4):
                        last = v_.tensor_scalar(qbd[s2][:, :, j, :], q_stack[s2][:], mm[:, j:j + 1], None, ALU.mult)
                    last.then_inc(qbd_ready, 1)
                if runs(v0, 0, steady):
                    dve.wait_ge(hi_ready, v + 1)
                    v_.tensor_tensor(qk_lo[s][:], qk[s][:], qk_hi[s][:], ALU.subtract).then_inc(lo_ready, 1)
                    for j in range(4):
                        last = v_.tensor_scalar(kbd[s][:, j, :], qk_hi[s][:, 1, :], mh[:, j:j + 1], None, ALU.mult)
                    last.then_inc(bd_ready, 1)
                if runs(v0, 3, steady) or runs(v0, 4, steady):
                    dve.wait_ge(pv_ps, v - 2)
                if runs(v0, 3, steady):
                    pv = psV[:, P:P + 272].rearrange("p (h b c) -> p h b c", h=8, b=2)
                    v_.reciprocal(rden[s3][:], pv[:, :, :, 16]).then_inc(rden_ready, 1)
                if runs(v0, 4, steady):
                    dve.wait_ge(res_ready, v - 3)
                    t = bass.ds(v - 4, 1)
                    v_.tensor_tensor(x1[:, t, :].rearrange("p a d -> p (a d)"), psV[:, 0:D],
                                     x_res[:, t, :].rearrange("p a d -> p (a d)"), ALU.add).then_inc(out_done, 1)
                if runs(v0, 3, steady):
                    dve.wait_ge(rden_ready, v - 2)
                    for h2 in range(2):
                        r = slice(64 * h2, 64 * h2 + 64)
                        for b in range(2):
                            last = v_.tensor_tensor(att[s3][64 * b:64 * b + 64, :, h2, :],
                                                    pv[r, :, b, 8 * h2:8 * h2 + 8],
                                                    rden[s3][r, :, b:b + 1].to_broadcast([64, 8, 8]), ALU.mult)
                    last.then_inc(att_ready, 1)

            dve.wait_ge(pool_const, 1 + 5 * SLOTS)
            steps(dve, step)

        @block.scalar
        def _(act):
            a = nc.scalar
            a.dma_start(cst[:], consts).then_inc(c_in, 16)
            a.dma_start(bo_row[:], bo.to_broadcast([P, D])).then_inc(c_in, 16)
            act.wait_ge(pool_const, 1)
            a.activation(act_warm[:], half[:, 0:1], ACT.Exp)
            act.wait_ge(c_in, 32)
            act.wait_ge(const_ready, 11)
            act.wait_ge(pool_const, 1 + 5 * SLOTS)

            def step(v, v0, steady=False):
                s, s1, s2, s3 = v0 % SLOTS, (v0 - 1) % SLOTS, (v0 - 2) % SLOTS, (v0 - 3) % SLOTS
                if runs(v0, 0, steady):
                    act.wait_ge(xT_ps, v + 1)
                    a.copy(cols[s][:, 0, :], psA[:, 0:P]).then_inc(xT_sb, 1)
                if runs(v0, 3, steady):
                    act.wait_ge(t_ps, v - 2)
                    a.activation(pT[s3][:].rearrange("p g q -> p (g q)"), psT[:].rearrange("p a q -> p (a q)"),
                                 ACT.Exp).then_inc(exp_ready, 1)
                if runs(v0, 1, steady):
                    act.wait_ge(rep_ps, v)
                    a.copy(q_stack[s1][0:96], psR[0][0:96])
                    a.copy(k_stack[s1][0:96], psR[1][0:96]).then_inc(rep_sb, 1)
                if runs(v0, 0, steady):
                    act.wait_ge(qkv_ps, v + 1)
                    a.activation(qk[s][:, 1, :], psA[:, P:2 * P], ACT.Identity, bias=b_col[:, 1:2])
                    a.activation(qk[s][:, 0, :], psA[:, 0:P], ACT.Identity, bias=bq_s[:, 0:1],
                                 scale=SCALE).then_inc(qk_sb, 1)
                if runs(v0, 2, steady):
                    act.wait_ge(mT_ps, v - 1)
                    a.copy(q_stack[s2][96:P], psR[0][96:P].rearrange("p g q -> p (g q)")[:, 0:256].bitcast(F16)
                           .rearrange("p (g q) -> p g q", g=4)).then_inc(mT_sb, 1)
                if runs(v0, 4, steady):
                    act.wait_ge(attT_ps, v - 3)
                    a.copy(cols[(v0 - 4) % SLOTS][:, 1, :], psA[:, 3 * P:4 * P]).then_inc(attT_sb, 1)
                if runs(v0, 3, steady):
                    if v0 == 3:
                        for i in range(4):
                            act.wait_ge(wraw_in[i], 16)
                    at = bass.ds(v - 3, 1)
                    a.copy(w_hi[:, at, :].rearrange("p a d -> p (a d)"),
                           w_raw[:, at, :].rearrange("p a d -> p (a d)")).then_inc(hi_split, 1)
                if runs(v0, 0, steady):
                    if v0 >= SLOTS:
                        act.wait_ge(pv_ps, v - 2)
                    for b in range(2):
                        r = slice(64 * b, 64 * b + 64)
                        ins = a.copy(vbd[s][r, b, :, 0:16],
                                     psA[r, 2 * P:3 * P].rearrange("p (h c) -> p h c", h=8))
                    ins.then_inc(v_sb, 1)

            steps(act, step)

        @block.tensor
        def _(pe):
            t_ = nc.tensor
            pe.wait_ge(warm_ready, 1)
            for _ in range(WARM):
                t_.matmul(psS[:, 0, :], warm[:, 0:P], warm[:], start=True, stop=True)
            pe.wait_ge(w_in, 16)
            pe.wait_ge(const_ready, 11)
            t_.matmul(psV[:, 0:D], bv_mat[:], w[:, 3, :], start=True, stop=True).then_inc(bvo_ps, 1)

            def scores(v, v0, lag, h):
                s1 = (v0 - lag) % SLOTS
                if h == 0:
                    pe.wait_ge(bd_ready, v)
                if v0 > lag or h:
                    pe.wait_ge(max_ready, 2 * v + (h - 2 * lag))
                for gl in range(2):
                    g0 = 32 * (2 * h + gl)
                    for b in range(2):
                        c = slice(64 * b, 64 * b + 64)
                        last = t_.matmul(psS[c, gl, 0:256], qk_hi[s1][g0:g0 + 32, 0, c],
                                         kbd[s1][g0:g0 + 32, :, c], start=True, stop=True)
                last.then_inc(s_ps, 1)

            def step(v, v0, steady=False):
                s, s1, s2, s3, s4 = (v0 % SLOTS, (v0 - 1) % SLOTS, (v0 - 2) % SLOTS, (v0 - 3) % SLOTS,
                                     (v0 - 4) % SLOTS)
                if runs(v0, 2, steady):
                    scores(v, v0, 2, 1)
                if runs(v0, 0, steady):
                    if v0 > 0:
                        pe.wait_ge(v_sb, v)
                    pe.wait_ge(xh_ready, v + 1)
                    t_.transpose(psA[:, 0:P], xh[s][:], id32).then_inc(xT_ps, 1)
                if runs(v0, 3, steady):
                    pe.wait_ge(qbd_ready, v - 2)
                    if v0 > 3:
                        pe.wait_ge(exp_ready, v - 3)
                    for g in range(4):
                        for b in range(2):
                            c = slice(64 * b, 64 * b + 64)
                            last = t_.matmul(psT[c, g // 2, 256 * (g % 2):256 * (g % 2) + 256],
                                             k_stack[s3][:, g, c], qbd[s3][:, g, :, c], start=True, stop=True)
                    last.then_inc(t_ps, 1)
                if runs(v0, 1, steady):
                    pe.wait_ge(lo_ready, v)
                    if v0 > 1:
                        pe.wait_ge(rep_sb, v - 1)
                    for i in range(2):
                        for g in range(4):
                            t_.matmul(psR[i][0:96, g, :], sel[:, 2 * i, g, :], qk_hi[s1][:, i, :],
                                      start=True, stop=False)
                            last = t_.matmul(psR[i][0:96, g, :], sel[:, 2 * i + 1, g, :], qk_lo[s1][:, i, :],
                                             start=False, stop=True)
                    last.then_inc(rep_ps, 1)
                if runs(v0, 0, steady):
                    pe.wait_ge(xT_sb, v + 1)
                    pe.wait_ge(ctx_in, 16 * v + 16)
                    t_.matmul(psA[:, 0:P], w[:, 0, :], cols[s][:, 0, :], start=True, stop=True)
                    t_.matmul(psA[:, P:2 * P], w[:, 1, :], ctx_sb[s][:], start=True, stop=True)
                    t_.matmul(psA[:, 2 * P:3 * P], ctx_sb[s][:], w[:, 2, :], start=True, stop=True).then_inc(qkv_ps, 1)
                if runs(v0, 2, steady):
                    pe.wait_ge(max_ready, 2 * v - 2)
                    if v0 > 2:
                        pe.wait_ge(mT_sb, v - 2)
                    mT = psR[0][96:P].rearrange("p g q -> p (g q)")[:, 0:256].bitcast(F16)
                    for g in range(4):
                        last = t_.transpose(mT[:, P * g:P * g + P], nmax[s2][:, g, :], id16[:])
                    last.then_inc(mT_ps, 1)
                if runs(v0, 1, steady):
                    scores(v, v0, 1, 0)
                def attend(pairs):
                    for hp in pairs:
                        last = t_.matmul(psV[:, P + 34 * hp:P + 34 * hp + 34],
                                         pT[s3][:, hp // 2, P * (hp % 2):P * (hp % 2) + P],
                                         vbd[s3][:, :, hp, :], start=True, stop=True)
                    return last

                if runs(v0, 3, steady):
                    pe.wait_ge(exp_ready, v - 2)
                    if v0 > 3:
                        pe.wait_ge(att_ready, v - 3)
                    attend(range(4))
                if runs(v0, 4, steady):
                    pe.wait_ge(att_ready, v - 3)
                    if runs(v0, 0, steady):
                        pe.wait_ge(qk_sb, v + 1)
                    else:
                        pe.wait_ge(v_sb, PAIRS)
                    if v0 > 4:
                        pe.wait_ge(attT_sb, v - 4)
                    t_.transpose(psA[:, 3 * P:4 * P], att[s4][:].rearrange("p h b c -> p (h b c)"),
                                 id32).then_inc(attT_ps, 1)
                if runs(v0, 3, steady):
                    last = attend(range(4, 8))
                if runs(v0, 4, steady):
                    pe.wait_ge(attT_sb, v - 3)
                    last = t_.matmul(psV[:, 0:P], cols[s4][:, 1, :], w[:, 3, :], start=True, stop=True)
                if runs(v0, 3, steady) or runs(v0, 4, steady):
                    last.then_inc(pv_ps, 1)

            steps(pe, step)


def experts(nc, x1, w_hi, w_lo, x2_rows, y_rows, rows, cols, b1, out):
    OUT_LAG = 5
    CODED = 8
    CODES = SLOT_TILES - CODED + 1
    with ExitStack() as stack:
        def sb(name, shape, dt=F32):
            return stack.enter_context(nc.sbuf_tensor(name, shape, dt))

        def pb(name, shape, dt=F32):
            return stack.enter_context(nc.psum_tensor(name, shape, dt))

        def sem(name):
            return stack.enter_context(nc.semaphore(name))

        E, U = EXPERTS, mybir.dt.uint32
        row_sb = sb("row_sb", [P, ROW_WIDTH])
        ln_w, ln_b, r_b, upto_e, mult128, count, b2_all = (
            row_sb[:, a:b] for a, b in zip(ROW_AT[:-1], ROW_AT[1:]))
        col_sb = sb("col_sb", [P, P + E + P + 1 + SLOT_TILES])
        id32, r_w, before = col_sb[:, 0:P], col_sb[:, P:P + E], col_sb[:, P + E:2 * P + E]
        row_no, empty_row = col_sb[:, 2 * P + E:2 * P + E + 1], col_sb[:, 2 * P + E + 1:]
        b1_sb = sb("b1_sb", [P, E, FC])
        half = sb("f_half", [P, PAIRS])
        mraw = sb("mraw", [P, PAIRS, 6])
        mv = sb("f_mv", [P, PAIRS, 2])
        veps = sb("f_veps", [P, PAIRS])
        rstd = sb("f_rstd", [P, PAIRS])
        x2 = sb("x2", [P, PAIRS, D])
        xT = sb("xT", [P, TOKENS])
        logits = sb("logits", [P, PAIRS, E])
        top = sb("top", [P, PAIRS, 8])
        top_i = sb("top_i", [P, PAIRS, 8], U)
        top_f = sb("top_f", [P, PAIRS, 2])
        gap = sb("gap", [P, PAIRS])
        ratio = sb("ratio", [P, PAIRS])
        denom = sb("denom", [P, PAIRS])
        wt = sb("wt", [P, 2, PAIRS])
        chosen = [sb(f"chosen{i}", [P, PAIRS, E]) for i in range(2)]
        both = sb("both", [P, PAIRS, E], F16)
        before16 = sb("before16", [P, P], F16)
        ones16 = sb("ones16", [P, P], F16)
        load = sb("load", [P, E])
        fills = sb("fills", [P, E, PAIRS])
        tiles = sb("tiles", [P, E])
        tiles_upto = sb("tiles_upto", [P, E, E])
        ends = sb("ends", [P, E])
        base = sb("base", [P, E])
        slot = sb("slot", [P, PAIRS, E])
        slot_of = [sb(f"slot_of{i}", [P, PAIRS, E]) for i in range(2)]
        pos = sb("pos", [P, 2, PAIRS])
        pos_i = sb("pos_i", [P, 2 * PAIRS], U)
        at_i = sb("at_i", [P, 2, 2 * PAIRS], U)
        at_f = sb("at_f", [P, 2, 2 * PAIRS], F16)
        count16 = sb("count16", [P, P], F16)
        passed = sb("passed", [P, SLOT_TILES, E])
        e_f = sb("e_f", [P, SLOT_TILES])
        e_min = sb("e_min", [P, SLOT_TILES])
        codes = [sb(f"codes{i}", [P, CODES]) for i in range(2)]
        e_code = sb("e_code", [P, CODES], mybir.dt.int32)
        in_row = sb("in_row", [P, 2 * PAIRS, P], F16)
        in_tile = sb("in_tile", [P, 3, 2 * PAIRS, SLOT_TILES], F16)
        found = sb("found", [P, 3, SLOT_TILES])
        src = sb("src", [P, SLOT_TILES], U)
        dst = sb("dst", [P, SLOT_TILES], U)
        row_of = sb("row_of", [P, SLOT_TILES])
        second = sb("second", [P, SLOT_TILES])
        empty = sb("empty", [P, SLOT_TILES])
        xg = [sb(f"xg{i}", [P, D]) for i in range(3)]
        xg_hi = [sb(f"xg_hi{i}", [P, P], F16) for i in range(3)]
        xg_lo = [sb(f"xg_lo{i}", [P, P], F16) for i in range(3)]
        b1_now = [sb(f"b1_now{i}", [P, FC]) for i in range(3)]
        h = [sb(f"h{i}", [P, FC * P]) for i in range(3)]
        h_hi = [sb(f"h_hi{i}", [P, FC * P], F16) for i in range(3)]
        h_lo = [sb(f"h_lo{i}", [P, FC * P], F16) for i in range(3)]
        y = [sb(f"y{i}", [P, D]) for i in range(3)]
        y_back = sb("y_back", [P, 2, PAIRS, D])
        mixed = sb("mixed", [P, PAIRS, D])
        oraw = sb("oraw", [P, PAIRS, 6])
        omv = sb("omv", [P, PAIRS, 2])
        oveps = sb("oveps", [P, PAIRS])
        orstd = sb("orstd", [P, PAIRS])
        onmean = sb("onmean", [P, PAIRS])
        onmr = sb("onmr", [P, PAIRS])
        normed = sb("normed", [P, PAIRS, D])
        scaled = sb("scaled", [P, PAIRS, D])

        psM = pb("psM", [P, 4, P])
        psX = pb("psX", [P, 512])
        psH = [pb(f"psH{i}", [P, FC * P]) for i in range(3)]
        psY = [pb(f"psY{i}", [P, 512]) for i in range(3)]

        row_in = sem("row_in")
        col_in = sem("col_in")
        bias_in = sem("bias_in")
        half_set = sem("half_set")
        raw_done = sem("raw_done")
        mv_ready = sem("mv_ready")
        veps_ready = sem("veps_ready")
        rstd_ready = sem("f_rstd_ready")
        x2_ready = sem("x2_ready")
        x2_stored = sem("x2_stored")
        x2T_ps = sem("x2T_ps")
        xT_ready = sem("xT_ready")
        logits_ps = sem("logits_ps")
        consts16 = sem("consts16")
        route = sem("route")
        gap_ready = sem("gap_ready")
        ratio_ready = sem("ratio_ready")
        both_ready = sem("both_ready")
        slot_ps = sem("slot_ps")
        tab_ready = sem("tab_ready")
        where_ready = sem("where_ready")
        found_ps = sem("found_ps")
        where_known = sem("where_known")
        xg_in = [sem(f"xg_in{i}") for i in range(3)]
        xg_ps = sem("xg_ps")
        xghi_ready = sem("xghi_ready")
        xg_ready = sem("xg_ready")
        b1_ready = sem("b1_ready")
        h_ps = sem("h_ps")
        gelu_ready = sem("gelu_ready")
        hhi_ready = sem("hhi_ready")
        h_ready = sem("h_ready")
        y_ps = sem("y_ps")
        y_ready = sem("y_ready")
        y_out = [sem(f"y_out{i}") for i in range(3)]
        back_in = [sem(f"back_in{k}") for k in range(BLOCKS)]
        first_added = sem("first_added")
        mixed_ready = sem("mixed_ready")
        oraw_done = sem("oraw_done")
        omv_ready = sem("omv_ready")
        oveps_ready = sem("oveps_ready")
        orstd_ready = sem("orstd_ready")
        onmr_ready = sem("onmr_ready")
        normed_ready = sem("normed_ready")
        scaled_ready = sem("scaled_ready")
        x1b_ready = sem("x1b_ready")
        result_ready = sem("result_ready")
        stored = sem("stored")

        FIRST, LAST, GROUP = 9, SLOT_TILES, 6

        def steps(engine, step, end):
            for v in range(FIRST):
                step(v, v, 0)
            with engine.Fori(0, (LAST - FIRST) // GROUP) as i:
                for k in range(GROUP):
                    step(i * GROUP + (FIRST + k), FIRST + k, i)
            for v in range(LAST, end):
                step(v, v, 0)

        def runs(v0, lag):
            return FIRST <= v0 < FIRST + GROUP or 0 <= v0 - lag < SLOT_TILES

        def first_coded(v0):
            first = v0 - (v0 - FIRST) % GROUP - OUT_LAG
            return first if FIRST <= v0 < LAST else min(max(first, 0), CODES - 1)

        def asks(v0):
            return v0 == 0 or (v0 - FIRST) % GROUP == 0

        def coded(engine, v, v0):
            at = v - OUT_LAG if FIRST <= v0 < LAST else first_coded(v0)
            return engine.value_load(e_code[0:1, bass.ds(at, 1)], min_val=0, max_val=E ** CODED - 1)

        def expert_of(code, v0, lag):
            return (code >> (3 * (v0 - lag - first_coded(v0)))) & (E - 1)

        def uses(v0, lag, i):
            return i * (GROUP // 3) + (v0 - lag) // 3

        block = stack.enter_context(nc.Block())
        out_t = out.rearrange("(t p) d -> p t d", p=P)
        x2_t = x2_rows.rearrange("(t p) d -> p t d", p=P)
        y_t = y_rows[0:2 * TOKENS].rearrange("(i t p) d -> p i t d", p=P, i=2)

        def quad(k):
            return slice(BT * k, BT * k + BT)

        @block.sync
        def _(sp):
            sp.dma_start(col_sb[:], cols).then_inc(col_in, 16)
            sp.dma_start(row_sb[:], rows.to_broadcast([P, ROW_WIDTH])).then_inc(row_in, 16)
            sp.dma_start(b1_sb[:], b1).then_inc(bias_in, 16)
            for k in range(BLOCKS):
                sp.wait_ge(x2_ready, BT * (k + 1))
                sp.dma_start(x2_t[:, quad(k), :], x2[:, quad(k), :]).then_inc(x2_stored, 16)
            for i in range(3):
                sp.wait_ge(y_out[i], 16 * len(range(i, SLOT_TILES, 3)))
            for k in range(BLOCKS):
                for i in range(2):
                    sp.dma_start(y_back[:, i, quad(k), :], y_t[:, i, quad(k), :]).then_inc(back_in[k], 16)
            for k in range(BLOCKS):
                sp.wait_ge(result_ready, k + 1)
                sp.dma_start(out_t[:, quad(k), :], x1[:, quad(k), :]).then_inc(stored, 16)
            sp.wait_ge(stored, 16 * BLOCKS)

        def scale(k):
            nc.gpsimd.wait_ge(normed_ready, k + 1)
            nc.gpsimd.tensor_tensor(scaled[:, quad(k), :], normed[:, quad(k), :],
                                    ln_w.unsqueeze(1).to_broadcast([P, BT, D]), ALU.mult).then_inc(scaled_ready, 1)

        @block.gpsimd
        def _(pool):
            g = nc.gpsimd
            g.memset(half[:], -0.5).then_inc(half_set, 1)
            pool.wait_ge(half_set, 1)
            for k in range(BLOCKS):
                t = quad(k)
                pool.wait_ge(mv_ready, BT * (k + 1))
                g.tensor_scalar(veps[:, t], mv[:, t, 1], EPS_IN, 1.0, ALU.add, ALU.mult).then_inc(veps_ready, 1)
                pool.wait_ge(veps_ready, k + 1)
                g.tensor_tensor(rstd[:, t], veps[:, t], half[:, t], ALU.pow).then_inc(rstd_ready, 1)
            pool.wait_ge(row_in, 16)
            pool.wait_ge(x2_ready, PAIRS)
            for t in range(PAIRS):
                g.tensor_tensor(x1[:, t, :], x1[:, t, :], ln_b, ALU.add).then_inc(x1b_ready, 1)
            pool.wait_ge(x2_stored, 16 * BLOCKS)

            pool.wait_ge(where_known, 2)

            for v in range(SLOT_TILES + OUT_LAG + 1):
                if v < SLOT_TILES:
                    r = v % 3
                    if v >= 3:
                        pool.wait_ge(xg_ps, v - 2)
                    g.indirect_dma_start(xg[r][:], None, x2_rows,
                                         bass.IndirectOffsetOnAxis(src[:, v:v + 1], 0)).then_inc(xg_in[r], 16)
                u = v - OUT_LAG - 1
                if u >= 0:
                    pool.wait_ge(y_ready, u + 1)
                    g.indirect_dma_start(y_rows, bass.IndirectOffsetOnAxis(dst[:, u:u + 1], 0),
                                         y[u % 3][:], None).then_inc(y_out[u % 3], 16)
            for k in range(BLOCKS):
                t = quad(k)
                pool.wait_ge(omv_ready, BT * (k + 1))
                g.tensor_scalar(oveps[:, t], omv[:, t, 1], EPS_OUT, 1.0, ALU.add, ALU.mult).then_inc(oveps_ready, 1)
                g.tensor_scalar(onmean[:, t], omv[:, t, 0], -1.0, 1.0, ALU.mult, ALU.mult).then_inc(oveps_ready, 1)
                pool.wait_ge(oveps_ready, 2 * k + 2)
                g.tensor_tensor(orstd[:, t], oveps[:, t], half[:, t], ALU.pow).then_inc(orstd_ready, 1)
                pool.wait_ge(orstd_ready, k + 1)
                g.tensor_tensor(onmr[:, t], onmean[:, t], orstd[:, t], ALU.mult).then_inc(onmr_ready, 1)
                if k:
                    scale(k - 1)
            scale(BLOCKS - 1)

        @block.vector
        def _(dve):
            v_ = nc.vector
            done = [0]

            def chained(ins):
                done[0] += 1
                ins.then_inc(route, 1)

            def all_before():
                dve.wait_ge(route, done[0])

            for t in range(PAIRS):
                v_.bn_stats(mraw[:, t, :], x1[:, t, :]).then_inc(raw_done, 1)
            for t in range(PAIRS):
                dve.wait_ge(raw_done, t + 1)
                v_.bn_aggr(mv[:, t, :], mraw[:, t, :]).then_inc(mv_ready, 1)
            for k in range(BLOCKS):
                dve.wait_ge(rstd_ready, k + 1)
                for t in range(BT * k, BT * k + BT):
                    v_.tensor_scalar(x2[:, t, :], x1[:, t, :], mv[:, t, 0:1], rstd[:, t:t + 1],
                                     ALU.subtract, ALU.mult).then_inc(x2_ready, 1)
            dve.wait_ge(row_in, 16)
            dve.wait_ge(col_in, 16)
            v_.tensor_copy(before16[:], before).then_inc(consts16, 1)
            v_.memset(ones16[:], 1.0).then_inc(consts16, 1)
            v_.tensor_copy(count16[:], count).then_inc(consts16, 1)
            dve.wait_ge(logits_ps, BLOCKS)
            chained(v_.tensor_tensor(logits[:], psM[:, 0, :].rearrange("p (t e) -> p t e", e=E),
                                     r_b.unsqueeze(1).to_broadcast([P, PAIRS, E]), ALU.add))
            all_before()
            for t in range(PAIRS):
                chained(v_.max(top[:, t, :], logits[:, t, :]))
            for t in range(PAIRS):
                dve.wait_ge(route, 2 + t)
                chained(v_.max_index(top_i[:, t, :], top[:, t, :], logits[:, t, :]))
            v_.tensor_tensor(gap[:], top[:, :, 1], top[:, :, 0], ALU.subtract).then_inc(gap_ready, 1)
            all_before()
            chained(v_.tensor_copy(top_f[:], top_i[:, :, 0:2]))
            all_before()
            for i in range(2):
                chained(v_.tensor_tensor(chosen[i][:], top_f[:, :, i:i + 1].to_broadcast([P, PAIRS, E]),
                                         count[:, 0:E].unsqueeze(1).to_broadcast([P, PAIRS, E]), ALU.is_equal))
            all_before()
            v_.tensor_tensor(both[:], chosen[0][:], chosen[1][:], ALU.add).then_inc(both_ready, 1)
            dve.wait_ge(ratio_ready, 1)
            chained(v_.tensor_scalar(denom[:], ratio[:], 1.0, None, ALU.add))
            all_before()
            chained(v_.reciprocal(wt[:, 0, :], denom[:]))
            all_before()
            chained(v_.tensor_tensor(wt[:, 1, :], wt[:, 0, :], ratio[:], ALU.mult))
            dve.wait_ge(slot_ps, 1)
            chained(v_.tensor_reduce(load[:], psM[:, 2, :].rearrange("p (t e) -> p e t", e=E), AX.X, ALU.add))
            all_before()
            chained(v_.tensor_tensor(fills[:], load[:].unsqueeze(2).to_broadcast([P, E, PAIRS]),
                                     mult128.unsqueeze(1).to_broadcast([P, E, PAIRS]), ALU.is_gt))
            all_before()
            chained(v_.tensor_reduce(tiles[:], fills[:], AX.X, ALU.add))
            all_before()
            chained(v_.tensor_tensor(tiles_upto[:], tiles[:].unsqueeze(1).to_broadcast([P, E, E]),
                                     upto_e.rearrange("p (a b) -> p a b", a=E), ALU.mult))
            all_before()
            chained(v_.tensor_reduce(ends[:], tiles_upto[:], AX.X, ALU.add))
            all_before()
            chained(v_.tensor_tensor(base[:], ends[:], tiles[:], ALU.subtract))
            all_before()
            chained(v_.tensor_scalar(base[:], base[:], float(P), None, ALU.mult))
            all_before()
            chained(v_.tensor_tensor(slot[:], psM[:, 1, :].rearrange("p (t e) -> p t e", e=E),
                                     base[:].unsqueeze(1).to_broadcast([P, PAIRS, E]), ALU.add))
            all_before()
            for i in range(2):
                chained(v_.tensor_tensor(slot_of[i][:], slot[:], chosen[i][:], ALU.mult))
            all_before()
            for i in range(2):
                chained(v_.tensor_reduce(pos[:, i, :], slot_of[i][:], AX.X, ALU.add))
            all_before()
            chained(v_.tensor_copy(pos_i[:], pos[:].rearrange("p i t -> p (i t)")))
            all_before()
            chained(v_.tensor_scalar(at_i[:, 0, :], pos_i[:], 7, None, ALU.logical_shift_right))
            chained(v_.tensor_scalar(at_i[:, 1, :], pos_i[:], P - 1, None, ALU.bitwise_and))
            all_before()
            chained(v_.tensor_copy(at_f[:], at_i[:]))
            dve.wait_ge(consts16, 3)
            all_before()
            C = 2 * PAIRS
            chained(v_.tensor_tensor(in_tile[:, 0], at_f[:, 0, :].unsqueeze(2).to_broadcast([P, C, SLOT_TILES]),
                                     count16[:, 0:SLOT_TILES].unsqueeze(1).to_broadcast([P, C, SLOT_TILES]),
                                     ALU.is_equal))
            all_before()
            chained(v_.tensor_scalar(in_tile[:, 1], in_tile[:, 0], row_no, None, ALU.mult))
            v_.tensor_tensor(in_tile[:, 2], in_tile[:, 0],
                             count16[:, 0:C].unsqueeze(2).to_broadcast([P, C, SLOT_TILES]),
                             ALU.mult).then_inc(where_ready, 1)
            for q in range(4):
                c = slice(q * C // 4, (q + 1) * C // 4)
                v_.tensor_tensor(in_row[:, c, :], at_f[:, 1, c].unsqueeze(2).to_broadcast([P, C // 4, P]),
                                 count16[:].unsqueeze(1).to_broadcast([P, C // 4, P]),
                                 ALU.is_equal).then_inc(where_ready, 1)
            chained(v_.tensor_tensor(passed[:], count[:, 0:SLOT_TILES].unsqueeze(2).to_broadcast([P, SLOT_TILES, E]),
                                     ends[:].unsqueeze(1).to_broadcast([P, SLOT_TILES, E]), ALU.is_ge))
            all_before()
            chained(v_.tensor_reduce(e_f[:], passed[:], AX.X, ALU.add))
            all_before()
            chained(v_.tensor_scalar(e_min[:], e_f[:], float(E - 1), None, ALU.min))
            all_before()
            for i in range(CODED - 1):
                first = codes[(i + 1) % 2][:] if i else e_min[:, CODED - 1:]
                ins = v_.scalar_tensor_tensor(e_code[:] if i == CODED - 2 else codes[i % 2][:], first, float(E),
                                              e_min[:, CODED - 2 - i:CODED - 2 - i + CODES], ALU.mult, ALU.add)
                if i == CODED - 2:
                    ins.then_inc(tab_ready, 1)
                else:
                    chained(ins)
                    all_before()
            dve.wait_ge(found_ps, 1)
            chained(v_.tensor_copy(found[:], psM[:, 3, 0:3 * SLOT_TILES].rearrange("p (a j) -> p a j", a=3)))
            all_before()
            chained(v_.scalar_tensor_tensor(row_of[:], found[:, 2, :], float(P), found[:, 1, :], ALU.mult, ALU.add))
            chained(v_.tensor_scalar(empty[:], found[:, 0, :], -1.0, 1.0, ALU.mult, ALU.add))
            all_before()
            chained(v_.tensor_scalar(second[:], row_of[:], float(TOKENS), float(TOKENS), ALU.is_ge, ALU.mult))
            chained(v_.tensor_tensor(empty[:], empty[:], empty_row, ALU.mult))
            all_before()
            v_.tensor_tensor(src[:], row_of[:], second[:], ALU.subtract).then_inc(where_known, 1)
            v_.tensor_tensor(dst[:], row_of[:], empty[:], ALU.add).then_inc(where_known, 1)
            dve.wait_ge(tab_ready, 1)

            code = [0]

            def step(v, v0, i):
                if asks(v0):
                    code[0] = coded(v_, v, v0)
                if runs(v0, 2):
                    r = (v0 - 2) % 3
                    dve.wait_ge(xg_ps, v - 1)
                    v_.tensor_copy(xg_hi[r][:], psX[:, 0:P]).then_inc(xghi_ready, 1)
                    dve.wait_ge(xghi_ready, v - 1)
                    v_.tensor_tensor(xg_lo[r][:], psX[:, 0:P], xg_hi[r][:], ALU.subtract).then_inc(xg_ready, 1)
                if runs(v0, 3):
                    r = v0 % 3
                    dve.wait_ge(gelu_ready, v - 2)
                    v_.tensor_copy(h_hi[r][:], h[r][:]).then_inc(hhi_ready, 1)
                    dve.wait_ge(hhi_ready, v - 2)
                    v_.tensor_tensor(h_lo[r][:], h[r][:], h_hi[r][:], ALU.subtract).then_inc(h_ready, 1)
                if runs(v0, OUT_LAG):
                    r = (v0 - OUT_LAG) % 3
                    expert = expert_of(code[0], v0, OUT_LAG)
                    dve.wait_ge(y_ps, v - (OUT_LAG - 1))
                    if v0 >= OUT_LAG + 3:
                        dve.wait_ge(y_out[r], uses(v0, OUT_LAG, i) * 16)
                    v_.tensor_tensor(y[r][:], psY[r][:, 0:D],
                                     b2_all.rearrange("p (e d) -> p e d", e=E)[:, bass.ds(expert, 1), :]
                                     .rearrange("p a d -> p (a d)"), ALU.add).then_inc(y_ready, 1)

            steps(dve, step, SLOT_TILES + OUT_LAG)

            def finish(k):
                dve.wait_ge(scaled_ready, k + 1)
                v_.tensor_tensor(x1[:, quad(k), :], x1[:, quad(k), :], scaled[:, quad(k), :],
                                 ALU.add).then_inc(result_ready, 1)

            dve.wait_ge(x1b_ready, PAIRS)
            for k in range(BLOCKS):
                dve.wait_ge(back_in[k], 32)
                for i in range(2):
                    for t in range(BT * k, BT * k + BT):
                        if i:
                            dve.wait_ge(first_added, t + 1)
                        v_.scalar_tensor_tensor(mixed[:, t, :], y_back[:, i, t, :], wt[:, i, t:t + 1],
                                                mixed[:, t, :] if i else x2[:, t, :], ALU.mult,
                                                ALU.add).then_inc(mixed_ready if i else first_added, 1)
                for t in range(BT * k, BT * k + BT):
                    dve.wait_ge(mixed_ready, t + 1)
                    v_.bn_stats(oraw[:, t, :], mixed[:, t, :]).then_inc(oraw_done, 1)
                for t in range(BT * k, BT * k + BT):
                    dve.wait_ge(oraw_done, t + 1)
                    v_.bn_aggr(omv[:, t, :], oraw[:, t, :]).then_inc(omv_ready, 1)
                if k > 1:
                    finish(k - 2)
            finish(BLOCKS - 2)
            finish(BLOCKS - 1)

        @block.scalar
        def _(act):
            a = nc.scalar
            for k in range(BLOCKS):
                act.wait_ge(x2T_ps, k + 1)
                a.copy(xT[:, 512 * k:512 * k + 512], psH[k % 2][:]).then_inc(xT_ready, 1)
            act.wait_ge(gap_ready, 1)
            a.activation(ratio[:], gap[:], ACT.Exp).then_inc(ratio_ready, 1)
            act.wait_ge(bias_in, 16)
            act.wait_ge(tab_ready, 1)

            code = [0]

            def step(v, v0, i):
                if asks(v0):
                    code[0] = coded(a, v, v0)
                if not runs(v0, 3):
                    return
                r = v0 % 3
                expert = expert_of(code[0], v0, 3)
                a.copy(b1_now[r][:], b1_sb[:, bass.ds(expert, 1), :].rearrange("p a c -> p (a c)")).then_inc(b1_ready, 1)
                act.wait_ge(b1_ready, v - 2)
                act.wait_ge(h_ps, v - 2)
                for c in range(FC):
                    last = a.activation(h[r][:, P * c:P * c + P], psH[r][:, P * c:P * c + P], ACT.Gelu,
                                        bias=b1_now[r][:, c:c + 1])
                last.then_inc(gelu_ready, 1)

            steps(act, step, SLOT_TILES + 3)
            for k in range(BLOCKS):
                act.wait_ge(onmr_ready, k + 1)
                for t in range(BT * k, BT * k + BT):
                    last = a.activation(normed[:, t, :], mixed[:, t, :], ACT.Identity, bias=onmr[:, t:t + 1],
                                        scale=orstd[:, t:t + 1])
                last.then_inc(normed_ready, 1)

        @block.tensor
        def _(pe):
            t_ = nc.tensor
            pe.wait_ge(col_in, 16)
            for k in range(BLOCKS + 1):
                if k < BLOCKS:
                    if k >= 2:
                        pe.wait_ge(xT_ready, k - 1)
                    for t in range(BT * k, BT * k + BT):
                        pe.wait_ge(x2_ready, t + 1)
                        last = t_.transpose(psH[k % 2][:, P * (t % BT):P * (t % BT) + P], x2[:, t, :], id32)
                    last.then_inc(x2T_ps, 1)
                if k > 0:
                    pe.wait_ge(xT_ready, k)
                    for t in range(BT * k - BT, BT * k):
                        last = t_.matmul(psM[:, 0, E * t:E * t + E], xT[:, P * t:P * t + P], r_w,
                                         start=True, stop=True)
                    last.then_inc(logits_ps, 1)
            pe.wait_ge(consts16, 3)
            pe.wait_ge(both_ready, 1)
            t_.matmul(psM[:, 1, :], before16[:], both[:].rearrange("p t e -> p (t e)"), start=True, stop=False)
            for t in range(PAIRS - 1):
                t_.matmul(psM[:, 1, E * (t + 1):], ones16[:], both[:, t:t + 1, :].to_broadcast([P, PAIRS - 1 - t, E]),
                          start=False, stop=t == PAIRS - 2)
            t_.matmul(psM[:, 2, :], ones16[:], both[:].rearrange("p t e -> p (t e)"),
                      start=True, stop=True).then_inc(slot_ps, 1)
            C = 2 * PAIRS
            for c in range(C):
                if c % (C // 4) == 0:
                    pe.wait_ge(where_ready, 2 + c // (C // 4))
                last = t_.matmul(psM[:, 3, 0:3 * SLOT_TILES], in_row[:, c, :], in_tile[:, :, c, :],
                                 start=c == 0, stop=c == C - 1)
            last.then_inc(found_ps, 1)
            pe.wait_ge(tab_ready, 1)

            code = [0]

            def step(v, v0, i):
                if asks(v0):
                    code[0] = coded(t_, v, v0)
                if runs(v0, 2):
                    r = (v0 - 2) % 3
                    pe.wait_ge(xg_in[r], uses(v0, 2, i) * 16 + 16)
                    if v0 > 2:
                        pe.wait_ge(xg_ready, v - 2)
                    t_.transpose(psX[:, 0:P], xg[r][:], id32).then_inc(xg_ps, 1)
                if runs(v0, 3):
                    r = v0 % 3
                    expert = expert_of(code[0], v0, 3)
                    if v0 < FIRST or v0 >= LAST:
                        pe.wait_ge(xg_ready, v - 2)
                    if v0 >= 6:
                        pe.wait_ge(gelu_ready, v - 5)
                    for c in range(FC):
                        f = slice(P * c, P * c + P)
                        w1_hi = w_hi[:, bass.ds(expert * 2, 1), f].rearrange("p a f -> p (a f)")
                        w1_lo = w_lo[:, bass.ds(expert * 2, 1), f].rearrange("p a f -> p (a f)")
                        t_.matmul(psH[r][:, f], w1_hi, xg_hi[r][:], start=True, stop=False)
                        t_.matmul(psH[r][:, f], w1_hi, xg_lo[r][:], start=False, stop=False)
                        last = t_.matmul(psH[r][:, f], w1_lo, xg_hi[r][:], start=False, stop=True)
                    last.then_inc(h_ps, 1)
                if runs(v0, OUT_LAG):
                    r = (v0 - OUT_LAG) % 3
                    expert = expert_of(code[0], v0, OUT_LAG)
                    pe.wait_ge(h_ready, v - (OUT_LAG - 1))
                    if v0 >= OUT_LAG + 3:
                        pe.wait_ge(y_ready, v - (OUT_LAG + 2))
                    for c in range(FC):
                        f = slice(P * c, P * c + P)
                        w2_hi = w_hi[:, bass.ds(expert * 2 + 1, 1), f].rearrange("p a f -> p (a f)")
                        w2_lo = w_lo[:, bass.ds(expert * 2 + 1, 1), f].rearrange("p a f -> p (a f)")
                        t_.matmul(psY[r][:, 0:D], h_hi[r][:, f], w2_hi, start=c == 0, stop=False)
                        t_.matmul(psY[r][:, 0:D], h_hi[r][:, f], w2_lo, start=False, stop=False)
                        last = t_.matmul(psY[r][:, 0:D], h_lo[r][:, f], w2_hi, start=False, stop=c == FC - 1)
                    last.then_inc(y_ps, 1)

            steps(pe, step, SLOT_TILES + OUT_LAG)


def xattn_moe_kernel(nc, x, ctxT, w4, consts, bo, w_ffn, rows, cols, b1, out):
    with ExitStack() as stack:
        x1 = stack.enter_context(nc.sbuf_tensor("x1", [P, PAIRS, D], F32))
        w_hi = stack.enter_context(nc.sbuf_tensor("w_hi", [P, 2 * EXPERTS, 512], F16))
        w_lo = stack.enter_context(nc.sbuf_tensor("w_lo", [P, 2 * EXPERTS, 512], F16))
        x2_rows = nc.dram_tensor("x2_rows", (TOKENS, D), F32).ap()
        y_rows = nc.dram_tensor("y_rows", (2 * TOKENS + SLOT_TILES * P, D), F32).ap()
        attention(nc, x1, w_hi, w_lo, x, ctxT, w4, consts, bo, w_ffn)
        experts(nc, x1, w_hi, w_lo, x2_rows, y_rows, rows, cols, b1, out)


def kernel(**inputs):
    import numpy as np
    import concourse.bacc as bacc
    from concourse.bass_utils import run_bass_kernel_spmd

    d = {name: np.asarray(a) for name, a in inputs.items()}
    att = {name: d["L0_xattn_" + name] for name in ("Wq", "Wk", "Wv", "Wo", "bq", "bk", "bv", "bo")}
    ffn = {name: d["L0_ffn_" + name] for name in
           ("router_w", "router_b", "w1", "b1", "w2", "b2", "ln_w", "ln_b")}
    p = np.arange(P)
    f32 = np.float32
    eye = np.eye(P, dtype=f32)
    own_group = ((p[:, None] // HD) % 4 == np.arange(4)).astype(f32)
    own_row = (np.where(p[:, None] < 96, (p[:, None] // HD) % 4, p[:, None] - 96) == np.arange(4)).astype(f32)
    w1 = ffn["w1"].transpose(2, 0, 1)
    w2 = ffn["w2"].transpose(2, 0, 1).reshape(FC, P, EXPERTS, D).transpose(1, 2, 0, 3).reshape(P, EXPERTS, FF)
    arrays = {
        "x_rows": d["x"].reshape(TOKENS, D),
        "ctxT": d["ctx_1024"].reshape(TOKENS, D).T,
        "w4": np.stack([att[name].T for name in ("Wq", "Wk", "Wv", "Wo")], 1),
        "consts": np.concatenate([eye, own_group, own_row] + [att[b].reshape(D, 1) for b in ("bq", "bk", "bv")], 1),
        "bo": att["bo"].reshape(1, D),
        "w_ffn": np.stack([w1, w2], 2).reshape(P, 2 * EXPERTS, FF),
        "rows": np.concatenate([ffn["ln_w"], ffn["ln_b"], ffn["router_b"],
                                np.tri(EXPERTS, dtype=f32).ravel(), np.arange(PAIRS, dtype=f32) * P,
                                np.arange(P, dtype=f32), ffn["b2"].ravel()]).reshape(1, -1),
        "cols": np.concatenate([eye, ffn["router_w"].T, np.triu(np.ones((P, P), f32), 1), p[:, None].astype(f32),
                                (2 * TOKENS + p[:, None] + P * np.arange(SLOT_TILES)).astype(f32)], 1),
        "b1": ffn["b1"].reshape(EXPERTS, FC, P).transpose(2, 0, 1),
    }
    arrays = {name: np.ascontiguousarray(a) for name, a in arrays.items()}
    nc = bacc.Bacc("TRN2", target_bir_lowering=False, num_devices=1)
    args = [nc.dram_tensor(name, a.shape, mybir.dt.from_np(a.dtype), kind="ExternalInput").ap()
            for name, a in arrays.items()]
    out = nc.dram_tensor("out", (TOKENS, D), F32, kind="ExternalOutput").ap()
    xattn_moe_kernel(nc, *args, out)
    r = run_bass_kernel_spmd(nc, [arrays], core_ids=[0])
    return r.results[0]["out"].reshape(BATCH, SEQ, D)
```

```python
from contextlib import ExitStack

import concourse.bass as bass
from concourse import mybir

ALU = mybir.AluOpType
ACT = mybir.ActivationFunctionType
AX = mybir.AxisListType
F32 = mybir.dt.float32
F16 = mybir.dt.float16
BF16 = mybir.dt.bfloat16

P = 128
D = 128
HEADS = 16
HD = D // HEADS
BATCH, SEQ = 32, 64
TOKENS = BATCH * SEQ
PAIRS = TOKENS // P
SLOTS = 3
STAGES = 7
LAST_STAGE = 6
EXPERTS = 8
FF = 512
FC = FF // P
BLOCKS = TOKENS // 512
BT = 512 // P
EPS_OUT = 1e-12
SLOT_TILES = (2 * TOKENS) // P + EXPERTS - 1
ROW_AT = [0]
for width in (D, D, EXPERTS, EXPERTS * EXPERTS, PAIRS, P, EXPERTS * D):
    ROW_AT.append(ROW_AT[-1] + width)
ROW_WIDTH = ROW_AT[-1]
WARM = 10
FILL, FILL_TAIL = 1, 6
CHUNK = 4
SCALE = float(HD) ** -0.5
EPS_IN = 1e-5




def attention(nc, x1, x2, logits, top, top_i, consts16, w_hi, w_lo, row_sb, col_sb, b1_sb, x, ctxT, w4, consts, bo, w_ffn, rows, cols, b1,
              x2_rows):
    with ExitStack() as stack:
        def sb(name, shape, dt=F32):
            return stack.enter_context(nc.sbuf_tensor(name, shape, dt))

        def pb(name, shape, dt=F32):
            return stack.enter_context(nc.psum_tensor(name, shape, dt))

        def sem(name):
            return stack.enter_context(nc.semaphore(name))

        x_sb = sb("x_sb", [P, PAIRS, D])
        x_res = sb("x_res", [P, PAIRS, D])
        w_raw = sb("w_raw", [P, 2 * EXPERTS, 512])
        ctx_sb = [sb(f"ctx{i}", [P, P]) for i in range(SLOTS)]
        w = sb("w", [P, 4, D])
        cst = sb("cst", [P, P + 11])
        id32, mh, mm, b_col = cst[:, 0:P], cst[:, P:P + 4], cst[:, P + 4:P + 8], cst[:, P + 8:P + 11]
        bq_s = sb("bq_s", [P, 1])
        bo_row = sb("bo_row", [P, D])
        bv_mat = sb("bv_mat", [P, P])
        bvo = sb("bvo", [P, D])
        id16 = sb("id16", [P, P], F16)
        sel = sb("sel", [P, 4, 4, 96], F16)
        stats = sb("stats", [P, PAIRS, 6])
        mv = sb("mv", [P, PAIRS, 2])
        half = sb("half", [P, PAIRS])
        veps = sb("veps", [P, PAIRS])
        rstd = sb("rstd", [P, PAIRS])
        nmr = sb("nmr", [P, PAIRS])
        nmean = sb("nmean", [P, PAIRS])
        xh = [sb(f"xh{i}", [P, D]) for i in range(SLOTS)]
        xr = [sb(f"xr{i}", [P, D]) for i in range(SLOTS)]
        cols_sb = [sb(f"cols_sb{i}", [P, 3, P]) for i in range(SLOTS)]
        r_b = row_sb[:, ROW_AT[2]:ROW_AT[3]]
        r_w = col_sb[:, P:P + EXPERTS]
        x2_now = [sb(f"x2_now{i}", [P, D]) for i in range(SLOTS)]
        held = sb("held", [P, 1])
        raw2 = [sb(f"raw2_{i}", [P, 6]) for i in range(SLOTS)]
        mv2 = [sb(f"mv2_{i}", [P, 2]) for i in range(SLOTS)]
        veps2 = [sb(f"veps2_{i}", [P, 1]) for i in range(SLOTS)]
        rstd2 = [sb(f"rstd2_{i}", [P, 1]) for i in range(SLOTS)]
        qk = [sb(f"qk{i}", [P, 2, P]) for i in range(SLOTS)]
        qk_hi = [sb(f"qk_hi{i}", [P, 2, P], F16) for i in range(SLOTS)]
        qk_lo = [sb(f"qk_lo{i}", [P, 2, P], F16) for i in range(SLOTS)]
        kbd = [sb(f"kbd{i}", [P, 4, P], F16) for i in range(SLOTS)]
        q_stack = [sb(f"q_stack{i}", [P, 4, P], F16) for i in range(SLOTS)]
        k_stack = [sb(f"k_stack{i}", [P, 4, P], F16) for i in range(SLOTS)]
        qbd = [sb(f"qbd{i}", [P, 4, 4, P], F16) for i in range(SLOTS)]
        vbd = [sb(f"vbd{i}", [P, 2, 8, 17]) for i in range(SLOTS)]
        nmax = [sb(f"nmax{i}", [P, 4, 32], F16) for i in range(SLOTS)]
        pT = [sb(f"pT{i}", [P, 4, 256]) for i in range(SLOTS)]
        rden = [sb(f"rden{i}", [P, 8, 2]) for i in range(SLOTS)]
        att = [sb(f"att{i}", [P, 8, 2, HD]) for i in range(SLOTS)]

        psS = pb("psS", [P, 2, 512])
        psT = pb("psT", [P, 2, 512])
        psR = [pb("psRq", [P, 4, P]), pb("psRk", [P, 4, P])]
        psA = pb("psA", [P, 512])
        psV = pb("psV", [P, 512])

        act_warm = sb("act_warm", [P, 1])
        warm = sb("warm", [P, 512], BF16)
        warm_ready = sem("warm_ready")
        x_in = [sem(f"x_in{c}") for c in range(PAIRS // CHUNK)]
        wraw_in = [sem(f"wraw_in{i}") for i in range(4)]
        hi_split = sem("hi_split")
        lo_split = sem("lo_split")
        ctx_in = sem("ctx_in")
        w_in = sem("w_in")
        c_in = sem("c_in")
        const_ready = sem("const_ready")
        pool_const = sem("pool_const")
        stats_raw = sem("stats_raw")
        stats_ready = sem("stats_ready")
        rs = sem("rs")
        bvo_ps = sem("bvo_ps")
        bvo_sb = sem("bvo_sb")
        res_ready = sem("res_ready")
        xh_ready = sem("xh_ready")
        xr_ready = sem("xr_ready")
        xT_ps = sem("xT_ps")
        xT_sb = sem("xT_sb")
        attT_ps = sem("attT_ps")
        attT_sb = sem("attT_sb")
        lo_ready = sem("lo_ready")
        qkv_ps = sem("qkv_ps")
        qk_sb = sem("qk_sb")
        v_sb = sem("v_sb")
        bd_ready = sem("bd_ready")
        s_ps = sem("s_ps")
        max_ready = sem("max_ready")
        mT_ps = sem("mT_ps")
        rep_ps = sem("rep_ps")
        rep_sb = sem("rep_sb")
        mT_sb = sem("mT_sb")
        qbd_ready = sem("qbd_ready")
        hi_ready = sem("hi_ready")
        t_ps = sem("t_ps")
        exp_ready = sem("exp_ready")
        pv_ps = sem("pv_ps")
        rden_ready = sem("rden_ready")
        att_ready = sem("att_ready")
        out_done = sem("out_done")
        row_in = sem("row_in")
        col_in = sem("col_in")
        bias_in = sem("bias_in")
        raw2_done = sem("raw2_done")
        mv2_ready = sem("mv2_ready")
        veps2_ready = sem("veps2_ready")
        rstd2_ready = sem("rstd2_ready")
        x2_ready = sem("x2_ready")
        x2_kept = sem("x2_kept")
        logits_ready = sem("logits_ready")
        x2_stored = sem("x2_stored")
        top_ready = sem("top_ready")
        top_i_ready = sem("top_i_ready")

        x_t = x.rearrange("(t p) d -> p t d", p=P)

        block = stack.enter_context(nc.Block())

        def steps(engine, step):
            for v in range(STAGES):
                step(v, v)
            with engine.Fori(0, (PAIRS - STAGES) // SLOTS) as i:
                for k in range(SLOTS):
                    step(i * SLOTS + (STAGES + k), STAGES + k, True)
            for v in range(PAIRS, PAIRS + LAST_STAGE):
                step(v, v)

        def runs(v0, lag, steady):
            return steady or 0 <= v0 - lag < PAIRS

        @block.sync
        def _(sp):
            sp.dma_start(x_sb[:, 0:CHUNK, :], x_t[:, 0:CHUNK, :]).then_inc(x_in[0], 16)
            sp.dma_start(w[:], w4).then_inc(w_in, 16)
            sp.dma_start(ctx_sb[0][:], ctxT[:, 0:P]).then_inc(ctx_in, 16)
            for c in range(1, PAIRS // CHUNK):
                sp.dma_start(x_sb[:, c * CHUNK:(c + 1) * CHUNK, :],
                             x_t[:, c * CHUNK:(c + 1) * CHUNK, :]).then_inc(x_in[c], 16)
            for v in range(1, PAIRS):
                sp.wait_ge(ctx_in, 16 * v)
                if v >= SLOTS:
                    sp.wait_ge(qkv_ps, v - SLOTS + 1)
                sp.dma_start(ctx_sb[v % SLOTS][:], ctxT[:, v * P:(v + 1) * P]).then_inc(ctx_in, 16)
                if v == 1:
                    sp.dma_start(col_sb[:], cols).then_inc(col_in, 16)
                    sp.dma_start(row_sb[:], rows.to_broadcast([P, ROW_WIDTH])).then_inc(row_in, 16)
                    sp.dma_start(b1_sb[:], b1).then_inc(bias_in, 16)
                if v == 2:
                    for i in range(4):
                        sp.dma_start(w_raw[:, 4 * i:4 * i + 4, :], w_ffn[:, 4 * i:4 * i + 4, :]).then_inc(wraw_in[i], 16)
            x2_t = x2_rows.rearrange("(t p) d -> p t d", p=P)
            for k in range(BLOCKS):
                t = slice(BT * k, BT * k + BT)
                sp.wait_ge(x2_kept, BT * (k + 1))
                sp.dma_start(x2_t[:, t, :], x2[:, t, :]).then_inc(x2_stored, 16)
            sp.wait_ge(x2_stored, 16 * BLOCKS)
            sp.wait_ge(bias_in, 16)

        @block.gpsimd
        def _(pool):
            g = nc.gpsimd
            g.memset(half[:], -0.5).then_inc(pool_const, 1)
            for i in range(SLOTS):
                g.memset(vbd[i][:], 0.0).then_inc(pool_const, 1)
                g.memset(nmax[i][:], 0.0).then_inc(pool_const, 1)
            pool.wait_ge(pool_const, 1 + 2 * SLOTS)
            for i in range(SLOTS):
                g.memset(k_stack[i][96:P], 1.0).then_inc(pool_const, 1)
            pool.wait_ge(pool_const, 1 + 3 * SLOTS)
            for i in range(SLOTS):
                for b in range(2):
                    g.memset(vbd[i][64 * b:64 * b + 64, b, :, 16:17], 1.0).then_inc(pool_const, 1)
            pool.wait_ge(pool_const, 1 + 5 * SLOTS)
            def rstd_of(c):
                t = slice(c * CHUNK, (c + 1) * CHUNK)
                pool.wait_ge(stats_ready, (c + 1) * CHUNK)
                g.tensor_scalar(veps[:, t], mv[:, t, 1], EPS_IN, 1.0, ALU.add, ALU.mult).then_inc(rs, 1)
                g.tensor_scalar(nmean[:, t], mv[:, t, 0], -1.0, 1.0, ALU.mult, ALU.mult).then_inc(rs, 1)
                pool.wait_ge(rs, 4 * c + 2)
                g.tensor_tensor(rstd[:, t], veps[:, t], half[:, t], ALU.pow).then_inc(rs, 1)
                pool.wait_ge(rs, 4 * c + 3)
                g.tensor_tensor(nmr[:, t], nmean[:, t], rstd[:, t], ALU.mult).then_inc(rs, 1)
                pool.wait_ge(rs, 4 * c + 4)

            def normalise(v, s, reused):
                at = bass.ds(v, 1)
                g.tensor_tensor(xr[s][:], x_sb[:, at, :].rearrange("p a d -> p (a d)"),
                                rstd[:, at].to_broadcast([P, D]), ALU.mult).then_inc(xr_ready, 1)
                if reused:
                    pool.wait_ge(xT_ps, v - (SLOTS - 1))
                    pool.nop()
                pool.wait_ge(xr_ready, v + 1)
                pool.nop()
                g.tensor_tensor(xh[s][:], xr[s][:], nmr[:, at].to_broadcast([P, D]), ALU.add).then_inc(xh_ready, 1)

            def residual(v):
                at = bass.ds(v, 1)
                g.tensor_tensor(x_res[:, at, :].rearrange("p a d -> p (a d)"),
                                x_sb[:, at, :].rearrange("p a d -> p (a d)"), bvo[:], ALU.add).then_inc(res_ready, 1)

            def low_part(v):
                at = bass.ds(v, 1)
                pool.wait_ge(hi_split, v + 1)
                pool.nop()
                g.tensor_tensor(w_lo[:, at, :].rearrange("p a d -> p (a d)"),
                                w_raw[:, at, :].rearrange("p a d -> p (a d)"),
                                w_hi[:, at, :].rearrange("p a d -> p (a d)"), ALU.subtract).then_inc(lo_split, 1)

            def step(v, v0, steady=False):
                if runs(v0, 0, steady):
                    normalise(v, v0 % SLOTS, v0 >= SLOTS)
                    if 1 <= v0 < 1 + PAIRS // CHUNK - 1:
                        rstd_of(v0 - 1 + 1)
                if runs(v0, 5, steady):
                    s = (v0 - 5) % SLOTS
                    pool.wait_ge(veps2_ready, v - 4)
                    g.tensor_tensor(rstd2[s][:], veps2[s][:], half[:, 0:1], ALU.pow).then_inc(rstd2_ready, 1)
                if runs(v0, 3, steady):
                    if v0 == 3:
                        pool.wait_ge(bvo_sb, 1)
                    residual(v - 3)
                if runs(v0, 4, steady):
                    low_part(v - 4)

            rstd_of(0)
            steps(pool, step)

        @block.vector
        def _(dve):
            v_ = nc.vector
            v_.memset(warm[:], 0.0).then_inc(warm_ready, 1)

            def chunk_stats(c):
                dve.wait_ge(x_in[c], 16)
                for t in range(c * CHUNK, (c + 1) * CHUNK):
                    v_.bn_stats(stats[:, t, :], x_sb[:, t, :]).then_inc(stats_raw, 1)
                for t in range(c * CHUNK, (c + 1) * CHUNK):
                    dve.wait_ge(stats_raw, t + 1)
                    v_.bn_aggr(mv[:, t, :], stats[:, t, :]).then_inc(stats_ready, 1)

            chunk_stats(0)
            dve.wait_ge(c_in, 32)
            v_.tensor_copy(id16[:], id32).then_inc(const_ready, 1)
            v_.memset(sel[:], 0.0).then_inc(const_ready, 1)
            v_.memset(bv_mat[:], 1.0).then_inc(const_ready, 1)
            v_.tensor_scalar(bq_s[:], b_col[:, 0:1], SCALE, None, ALU.mult).then_inc(const_ready, 1)
            dve.wait_ge(const_ready, 4)
            for i, blocks in enumerate(((0, 2), (1,), (0, 1), (2,))):
                for k in blocks:
                    v_.tensor_copy(sel[:, i, :, 32 * k:32 * k + 32],
                                   id16[:].rearrange("p (g c) -> p g c", g=4)).then_inc(const_ready, 1)
            v_.tensor_scalar(bv_mat[:], bv_mat[:], b_col[:, 2:3], None, ALU.mult).then_inc(const_ready, 1)
            dve.wait_ge(bvo_ps, 1)
            v_.tensor_tensor(bvo[:], psV[:, 0:D], bo_row[:], ALU.add).then_inc(bvo_sb, 1)

            def largest_two(t0, t1):
                dve.wait_ge(logits_ready, t1)
                for t in range(t0, t1):
                    v_.max(top[:, t, :], logits[:, t, :]).then_inc(top_ready, 1)
                for t in range(t0, t1):
                    dve.wait_ge(top_ready, t + 1)
                    v_.max_index(top_i[:, t, :], top[:, t, :], logits[:, t, :]).then_inc(top_i_ready, 1)

            def step(v, v0, steady=False):
                s = v0 % SLOTS
                s2, s3 = (v0 - 2) % SLOTS, (v0 - 3) % SLOTS

                def largest(lag, h):
                    dve.wait_ge(s_ps, 2 * v + (1 + h - 2 * lag))
                    v_.tensor_reduce(nmax[(v0 - lag) % SLOTS][:, 2 * h:2 * h + 2, 0:4],
                                     psS[:, :, 0:256].rearrange("p g (h k) -> p g h k", h=4),
                                     AX.X, ALU.max, negate=True).then_inc(max_ready, 1)

                if runs(v0, 2, steady):
                    largest(2, 1)
                if runs(v0, 4, steady):
                    s4 = (v0 - 4) % SLOTS
                    pv = psV[:, P:P + 272].rearrange("p (h b c) -> p h b c", h=8, b=2)
                    dve.wait_ge(rden_ready, v - 3)
                    for h2 in range(2):
                        r = slice(64 * h2, 64 * h2 + 64)
                        for b in range(2):
                            last = v_.tensor_tensor(att[s4][64 * b:64 * b + 64, :, h2, :],
                                                    pv[r, :, b, 8 * h2:8 * h2 + 8],
                                                    rden[s4][r, :, b:b + 1].to_broadcast([64, 8, 8]), ALU.mult)
                    last.then_inc(att_ready, 1)
                if runs(v0, 5, steady):
                    s5, t = (v0 - 5) % SLOTS, bass.ds(v - 5, 1)
                    dve.wait_ge(rstd2_ready, v - 4)
                    v_.tensor_scalar(x2_now[s5][:],
                                     x1[:, t, :].rearrange("p a d -> p (a d)"), mv2[s5][:, 0:1], rstd2[s5][:],
                                     ALU.subtract, ALU.mult).then_inc(x2_ready, 1)
                if runs(v0, 1, steady):
                    largest(1, 0)
                if runs(v0, 0, steady):
                    dve.wait_ge(qk_sb, v + 1)
                    v_.tensor_copy(qk_hi[s][:], qk[s][:]).then_inc(hi_ready, 1)
                if runs(v0, 2, steady):
                    dve.wait_ge(mT_sb, v - 1)
                    for j in range(4):
                        last = v_.tensor_scalar(qbd[s2][:, :, j, :], q_stack[s2][:], mm[:, j:j + 1], None, ALU.mult)
                    last.then_inc(qbd_ready, 1)
                if runs(v0, 0, steady):
                    dve.wait_ge(hi_ready, v + 1)
                    v_.tensor_tensor(qk_lo[s][:], qk[s][:], qk_hi[s][:], ALU.subtract).then_inc(lo_ready, 1)
                    for j in range(4):
                        last = v_.tensor_scalar(kbd[s][:, j, :], qk_hi[s][:, 1, :], mh[:, j:j + 1], None, ALU.mult)
                    last.then_inc(bd_ready, 1)
                if 3 <= v0:
                    dve.wait_ge(pv_ps, v - 2)
                if runs(v0, 3, steady):
                    pv = psV[:, P:P + 272].rearrange("p (h b c) -> p h b c", h=8, b=2)
                    v_.reciprocal(rden[s3][:], pv[:, :, :, 16]).then_inc(rden_ready, 1)
                if runs(v0, 4, steady):
                    dve.wait_ge(res_ready, v - 3)
                    t = bass.ds(v - 4, 1)
                    v_.tensor_tensor(x1[:, t, :].rearrange("p a d -> p (a d)"), psV[:, 0:D],
                                     x_res[:, t, :].rearrange("p a d -> p (a d)"), ALU.add).then_inc(out_done, 1)
                if runs(v0, 6, steady):
                    t = bass.ds(v - 6, 1)
                    v_.tensor_tensor(logits[:, t, :].rearrange("p a e -> p (a e)"), psV[:, 400:400 + EXPERTS],
                                     r_b, ALU.add).then_inc(logits_ready, 1)
                if runs(v0, 4, steady):
                    s4, t = (v0 - 4) % SLOTS, bass.ds(v - 4, 1)
                    dve.wait_ge(out_done, v - 3)
                    v_.memset(held[:], 0.0)
                    v_.bn_stats(raw2[s4][:], x1[:, t, :].rearrange("p a d -> p (a d)")).then_inc(raw2_done, 1)
                    dve.wait_ge(raw2_done, v - 3)
                    v_.memset(held[:], 0.0)
                    v_.bn_aggr(mv2[s4][:], raw2[s4][:]).then_inc(mv2_ready, 1)
                    dve.wait_ge(mv2_ready, v - 3)
                    v_.tensor_scalar(veps2[s4][:], mv2[s4][:, 1:2], EPS_IN, None, ALU.add).then_inc(veps2_ready, 1)
                if v0 < PAIRS // CHUNK - 1:
                    chunk_stats(v0 + 1)
                if v0 == PAIRS:
                    v_.tensor_copy(consts16[:, 0, :], col_sb[:, P + EXPERTS:2 * P + EXPERTS])
                    v_.memset(consts16[:, 1, :], 1.0)
                    v_.tensor_copy(consts16[:, 2, :], row_sb[:, ROW_AT[5]:ROW_AT[6]])
                if PAIRS < v0 < PAIRS + 4:
                    largest_two(BT * (v0 - PAIRS - 1), BT * (v0 - PAIRS))
                if v0 == PAIRS + 4:
                    largest_two(BT * 3, BT * 3 + 2)

            dve.wait_ge(pool_const, 1 + 5 * SLOTS)
            dve.wait_ge(row_in, 16)
            dve.wait_ge(col_in, 16)
            steps(dve, step)
            largest_two(BT * 3 + 2, PAIRS)

        @block.scalar
        def _(act):
            a = nc.scalar
            a.dma_start(cst[:], consts).then_inc(c_in, 16)
            a.dma_start(bo_row[:], bo.to_broadcast([P, D])).then_inc(c_in, 16)
            act.wait_ge(pool_const, 1)
            a.activation(act_warm[:], half[:, 0:1], ACT.Exp)
            act.wait_ge(c_in, 32)
            act.wait_ge(const_ready, 11)
            act.wait_ge(pool_const, 1 + 5 * SLOTS)

            def stacks(v, v0):
                act.wait_ge(rep_ps, v)
                a.copy(q_stack[(v0 - 1) % SLOTS][0:96], psR[0][0:96])
                a.copy(k_stack[(v0 - 1) % SLOTS][0:96], psR[1][0:96]).then_inc(rep_sb, 1)

            def queries_keys(v, v0):
                act.wait_ge(qkv_ps, v + 1)
                a.activation(qk[v0 % SLOTS][:, 1, :], psA[:, P:2 * P], ACT.Identity, bias=b_col[:, 1:2])
                a.activation(qk[v0 % SLOTS][:, 0, :], psA[:, 0:P], ACT.Identity, bias=bq_s[:, 0:1],
                             scale=SCALE).then_inc(qk_sb, 1)

            def values(v, v0):
                if v0 >= SLOTS:
                    act.wait_ge(pv_ps, v - 2)
                for b in range(2):
                    r = slice(64 * b, 64 * b + 64)
                    ins = a.copy(vbd[v0 % SLOTS][r, b, :, 0:16],
                                 psA[r, 2 * P:3 * P].rearrange("p (h c) -> p h c", h=8))
                ins.then_inc(v_sb, 1)

            def step(v, v0, steady=False):
                s, s1, s2, s3 = v0 % SLOTS, (v0 - 1) % SLOTS, (v0 - 2) % SLOTS, (v0 - 3) % SLOTS
                if runs(v0, 0, steady):
                    act.wait_ge(xT_ps, v + 1)
                    a.copy(cols_sb[s][:, 0, :], psA[:, 0:P]).then_inc(xT_sb, 1)
                if runs(v0, 3, steady):
                    act.wait_ge(t_ps, v - 2)
                    a.activation(pT[s3][:].rearrange("p g q -> p (g q)"), psT[:].rearrange("p a q -> p (a q)"),
                                 ACT.Exp).then_inc(exp_ready, 1)
                if runs(v0, 1, steady):
                    stacks(v, v0)
                if runs(v0, 0, steady):
                    queries_keys(v, v0)
                    if v0 < SLOTS:
                        values(v, v0)
                if runs(v0, 2, steady):
                    act.wait_ge(mT_ps, v - 1)
                    a.copy(q_stack[s2][96:P], psR[0][96:P].rearrange("p g q -> p (g q)")[:, 0:256].bitcast(F16)
                           .rearrange("p (g q) -> p g q", g=4)).then_inc(mT_sb, 1)
                if runs(v0, 6, steady):
                    act.wait_ge(x2_ready, v - 5)
                    a.copy(x2[:, bass.ds(v - 6, 1), :].rearrange("p a d -> p (a d)"),
                           x2_now[v0 % SLOTS][:]).then_inc(x2_kept, 1)
                if v0 >= 4:
                    c0, c1 = (0 if runs(v0, 6, steady) else 1), (2 if runs(v0, 4, steady) else 1)
                    act.wait_ge(attT_ps, v - 3)
                    a.copy(cols_sb[s][:, 1 + c0:1 + c1, :],
                           psA[:].rearrange("p (c i d) -> p i c d", c=2, i=2)[:, 1, c0:c1, :]).then_inc(attT_sb, 1)
                if runs(v0, 3, steady):
                    if v0 - 3 < 4:
                        act.wait_ge(wraw_in[v0 - 3], 16)
                    at = bass.ds(v - 3, 1)
                    a.copy(w_hi[:, at, :].rearrange("p a d -> p (a d)"),
                           w_raw[:, at, :].rearrange("p a d -> p (a d)")).then_inc(hi_split, 1)
                if v0 >= SLOTS and runs(v0, 0, steady):
                    values(v, v0)

            steps(act, step)

        @block.tensor
        def _(pe):
            t_ = nc.tensor
            pe.wait_ge(warm_ready, 1)
            for _ in range(WARM):
                t_.matmul(psS[:, 0, :], warm[:, 0:P], warm[:], start=True, stop=True)
            pe.wait_ge(w_in, 16)
            pe.wait_ge(const_ready, 11)
            t_.matmul(psV[:, 0:D], bv_mat[:], w[:, 3, :], start=True, stop=True).then_inc(bvo_ps, 1)

            def scores(v, v0, lag, h):
                s1 = (v0 - lag) % SLOTS
                if h == 0:
                    pe.wait_ge(bd_ready, v)
                if v0 > lag or h:
                    pe.wait_ge(max_ready, 2 * v + (h - 2 * lag))
                for gl in range(2):
                    g0 = 32 * (2 * h + gl)
                    for b in range(2):
                        c = slice(64 * b, 64 * b + 64)
                        last = t_.matmul(psS[c, gl, 0:256], qk_hi[s1][g0:g0 + 32, 0, c],
                                         kbd[s1][g0:g0 + 32, :, c], start=True, stop=True)
                last.then_inc(s_ps, 1)

            def repeat_parts(v, v0):
                pe.wait_ge(lo_ready, v)
                if v0 > 1:
                    pe.wait_ge(rep_sb, v - 1)
                for i in range(2):
                    for g in range(4):
                        t_.matmul(psR[i][0:96, g, :], sel[:, 2 * i, g, :], qk_hi[(v0 - 1) % SLOTS][:, i, :],
                                  start=True, stop=False)
                        last = t_.matmul(psR[i][0:96, g, :], sel[:, 2 * i + 1, g, :], qk_lo[(v0 - 1) % SLOTS][:, i, :],
                                         start=False, stop=True)
                last.then_inc(rep_ps, 1)

            def project(v, v0):
                pe.wait_ge(xT_sb, v + 1)
                pe.wait_ge(ctx_in, 16 * v + 16)
                t_.matmul(psA[:, 0:P], w[:, 0, :], cols_sb[v0 % SLOTS][:, 0, :], start=True, stop=True)
                t_.matmul(psA[:, P:2 * P], w[:, 1, :], ctx_sb[v0 % SLOTS][:], start=True, stop=True)
                t_.matmul(psA[:, 2 * P:3 * P], ctx_sb[v0 % SLOTS][:], w[:, 2, :], start=True, stop=True).then_inc(qkv_ps, 1)

            def step(v, v0, steady=False):
                s, s1, s2, s3, s4 = (v0 % SLOTS, (v0 - 1) % SLOTS, (v0 - 2) % SLOTS, (v0 - 3) % SLOTS,
                                     (v0 - 4) % SLOTS)
                if runs(v0, 2, steady):
                    scores(v, v0, 2, 1)
                if runs(v0, 4, steady):
                    for _ in range(FILL if v0 < PAIRS else FILL_TAIL):
                        t_.matmul(psT[:, 0, :], warm[:, 0:P], warm[:], start=True, stop=True)
                if runs(v0, 0, steady):
                    if v0 > 0:
                        pe.wait_ge(v_sb, v)
                    pe.wait_ge(xh_ready, v + 1)
                    t_.transpose(psA[:, 0:P], xh[s][:], id32).then_inc(xT_ps, 1)
                if runs(v0, 3, steady):
                    pe.wait_ge(qbd_ready, v - 2)
                    if v0 > 3:
                        pe.wait_ge(exp_ready, v - 3)
                    for g in range(4):
                        for b in range(2):
                            c = slice(64 * b, 64 * b + 64)
                            last = t_.matmul(psT[c, g // 2, 256 * (g % 2):256 * (g % 2) + 256],
                                             k_stack[s3][:, g, c], qbd[s3][:, g, :, c], start=True, stop=True)
                    last.then_inc(t_ps, 1)
                if runs(v0, 1, steady):
                    repeat_parts(v, v0)
                if runs(v0, 0, steady):
                    project(v, v0)
                if runs(v0, 2, steady):
                    pe.wait_ge(max_ready, 2 * v - 2)
                    if v0 > 2:
                        pe.wait_ge(mT_sb, v - 2)
                    mT = psR[0][96:P].rearrange("p g q -> p (g q)")[:, 0:256].bitcast(F16)
                    for g in range(4):
                        last = t_.transpose(mT[:, P * g:P * g + P], nmax[s2][:, g, :], id16[:])
                    last.then_inc(mT_ps, 1)
                if runs(v0, 1, steady):
                    scores(v, v0, 1, 0)
                def attend(pairs):
                    for hp in pairs:
                        last = t_.matmul(psV[:, P + 34 * hp:P + 34 * hp + 34],
                                         pT[s3][:, hp // 2, P * (hp % 2):P * (hp % 2) + P],
                                         vbd[s3][:, :, hp, :], start=True, stop=True)
                    return last

                if runs(v0, 3, steady):
                    pe.wait_ge(exp_ready, v - 2)
                    if v0 > 3:
                        pe.wait_ge(att_ready, v - 3)
                    attend(range(4))
                if v0 >= 4:
                    if runs(v0, 0, steady):
                        pe.wait_ge(qk_sb, v + 1)
                    else:
                        pe.wait_ge(v_sb, PAIRS)
                    if v0 > 4:
                        pe.wait_ge(attT_sb, v - 4)
                if runs(v0, 6, steady):
                    pe.wait_ge(x2_ready, v - 5)
                    last = t_.transpose(psA[:, P:2 * P], x2_now[v0 % SLOTS][:], id32)
                if runs(v0, 4, steady):
                    pe.wait_ge(att_ready, v - 3)
                    last = t_.transpose(psA[:, 3 * P:4 * P], att[s4][:].rearrange("p h b c -> p (h b c)"), id32)
                if v0 >= 4:
                    last.then_inc(attT_ps, 1)
                if runs(v0, 3, steady):
                    last = attend(range(4, 8))
                if runs(v0, 4, steady):
                    pe.wait_ge(attT_sb, v - 3)
                    last = t_.matmul(psV[:, 0:P], cols_sb[s][:, 2, :], w[:, 3, :], start=True, stop=True)
                if runs(v0, 6, steady):
                    if v0 == 6:
                        pe.wait_ge(col_in, 16)
                    pe.wait_ge(attT_sb, v - 3)
                    if v0 > 19:
                        pe.wait_ge(logits_ready, v - 6)
                    last = t_.matmul(psV[:, 400:400 + EXPERTS], cols_sb[s][:, 1, :], r_w, start=True, stop=True)
                if v0 >= 3:
                    last.then_inc(pv_ps, 1)

            steps(pe, step)


def experts(nc, x1, x2, top, top_i, consts16, w_hi, w_lo, row_sb, col_sb, b1_sb, x2_rows, y_rows, out):
    GROUP = 6
    OUT_LAG = 5
    CODED = 8
    CODES = SLOT_TILES - CODED + 1
    with ExitStack() as stack:
        def sb(name, shape, dt=F32):
            return stack.enter_context(nc.sbuf_tensor(name, shape, dt))

        def pb(name, shape, dt=F32):
            return stack.enter_context(nc.psum_tensor(name, shape, dt))

        def sem(name):
            return stack.enter_context(nc.semaphore(name))

        E, U, C = EXPERTS, mybir.dt.uint32, 2 * PAIRS
        ln_w, ln_b, _, upto_e, mult128, count, b2_all = (
            row_sb[:, a:b] for a, b in zip(ROW_AT[:-1], ROW_AT[1:]))
        id32 = col_sb[:, 0:P]
        row_no, empty_row = col_sb[:, 2 * P + E:2 * P + E + 1], col_sb[:, 2 * P + E + 1:]
        half = sb("f_half", [P, PAIRS])
        top_f = sb("top_f", [P, PAIRS, 2])
        gap = sb("gap", [P, PAIRS])
        table_load = sb("table_load", [P, 1])
        ratio = sb("ratio", [P, PAIRS])
        denom = sb("denom", [P, PAIRS])
        wt = sb("wt", [P, 2, PAIRS])
        chosen = [sb(f"chosen{i}", [P, PAIRS, E]) for i in range(2)]
        both = sb("both", [P, PAIRS, E], F16)
        load = sb("load", [P, E])
        fills = sb("fills", [P, E, PAIRS])
        tiles = sb("tiles", [P, E])
        tiles_upto = sb("tiles_upto", [P, E, E])
        ends = sb("ends", [P, E])
        base = sb("base", [P, E])
        slot = sb("slot", [P, PAIRS, E])
        slot_of = [sb(f"slot_of{i}", [P, PAIRS, E]) for i in range(2)]
        pos = sb("pos", [P, 2, PAIRS])
        pos_i = sb("pos_i", [P, 2 * PAIRS], U)
        at_i = sb("at_i", [P, 2, 2 * PAIRS], U)
        at_f = sb("at_f", [P, 2, 2 * PAIRS], F16)
        before16, ones16, count16 = consts16[:, 0, :], consts16[:, 1, :], consts16[:, 2, :]
        passed = sb("passed", [P, SLOT_TILES, E])
        e_f = sb("e_f", [P, SLOT_TILES])
        e_min = sb("e_min", [P, SLOT_TILES])
        codes = [sb(f"codes{i}", [P, CODES]) for i in range(2)]
        e_code = sb("e_code", [P, CODES], mybir.dt.int32)
        in_row = sb("in_row", [P, 2 * PAIRS, P], F16)
        in_tile = sb("in_tile", [P, 3, 2 * PAIRS, SLOT_TILES], F16)
        found = sb("found", [P, 3, SLOT_TILES])
        src = sb("src", [P, SLOT_TILES], U)
        dst = sb("dst", [P, SLOT_TILES], U)
        row_of = sb("row_of", [P, SLOT_TILES])
        second = sb("second", [P, SLOT_TILES])
        empty = sb("empty", [P, SLOT_TILES])
        xg = [sb(f"xg{i}", [P, D]) for i in range(GROUP)]
        xg_hi = [sb(f"xg_hi{i}", [P, P], F16) for i in range(3)]
        xg_lo = [sb(f"xg_lo{i}", [P, P], F16) for i in range(3)]
        b1_now = [sb(f"b1_now{i}", [P, FC]) for i in range(3)]
        h = [sb(f"h{i}", [P, FC * P]) for i in range(3)]
        h_hi = [sb(f"h_hi{i}", [P, FC * P], F16) for i in range(3)]
        h_lo = [sb(f"h_lo{i}", [P, FC * P], F16) for i in range(3)]
        y = [sb(f"y{i}", [P, D]) for i in range(3)]
        y_back = sb("y_back", [P, 2, PAIRS, D])
        weighted = sb("weighted", [P, PAIRS, D])
        mixed = sb("mixed", [P, PAIRS, D])
        oraw = sb("oraw", [P, PAIRS, 6])
        omv = sb("omv", [P, PAIRS, 2])
        oveps = sb("oveps", [P, PAIRS])
        orstd = sb("orstd", [P, PAIRS])
        onmean = sb("onmean", [P, PAIRS])
        onmr = sb("onmr", [P, PAIRS])
        normed = sb("normed", [P, PAIRS, D])
        scaled = sb("scaled", [P, PAIRS, D])

        psM = pb("psM", [P, 4, P])
        psX = pb("psX", [P, 512])
        psH = [pb(f"psH{i}", [P, FC * P]) for i in range(3)]
        psY = [pb(f"psY{i}", [P, 512]) for i in range(3)]

        half_set = sem("half_set")
        route = sem("route")
        gap_ready = sem("gap_ready")
        ratio_ready = sem("ratio_ready")
        both_ready = sem("both_ready")
        slot_ps = sem("slot_ps")
        tab_ready = sem("tab_ready")
        where_ready = sem("where_ready")
        where_pool = sem("where_pool")
        plane_ready = sem("plane_ready")
        found_ps = sem("found_ps")
        where_known = sem("where_known")
        xg_in = [sem(f"xg_in{i}") for i in range(GROUP)]
        xb_ready = sem("xb_ready")
        xg_ps = sem("xg_ps")
        xghi_ready = sem("xghi_ready")
        xg_ready = sem("xg_ready")
        b1_ready = sem("b1_ready")
        h_ps = sem("h_ps")
        gelu_ready = sem("gelu_ready")
        hhi_ready = sem("hhi_ready")
        h_ready = sem("h_ready")
        y_ps = sem("y_ps")
        y_ready = sem("y_ready")
        y_out = [sem(f"y_out{i}") for i in range(3)]
        back_in = [sem(f"back_in{k}") for k in range(BLOCKS)]
        first_weighted = sem("first_weighted")
        mixed_ready = sem("mixed_ready")
        oraw_done = sem("oraw_done")
        omv_ready = sem("omv_ready")
        oveps_ready = sem("oveps_ready")
        orstd_ready = sem("orstd_ready")
        onmr_ready = sem("onmr_ready")
        normed_ready = sem("normed_ready")
        scaled_ready = sem("scaled_ready")
        third_scaled = sem("third_scaled")
        last_scaled = sem("last_scaled")
        x1b_ready = sem("x1b_ready")
        result_ready = sem("result_ready")
        stored = sem("stored")

        FIRST, LAST = 9, SLOT_TILES

        def steps(engine, step, end):
            for v in range(FIRST):
                step(v, v, 0)
            with engine.Fori(0, (LAST - FIRST) // GROUP) as i:
                for k in range(GROUP):
                    step(i * GROUP + (FIRST + k), FIRST + k, i)
            for v in range(LAST, end):
                step(v, v, 0)

        def runs(v0, lag):
            return FIRST <= v0 < FIRST + GROUP or 0 <= v0 - lag < SLOT_TILES

        def first_coded(v0):
            first = v0 - (v0 - FIRST) % GROUP - OUT_LAG
            return first if FIRST <= v0 < LAST else min(max(first, 0), CODES - 1)

        def asks(v0):
            return v0 == 0 or (v0 - FIRST) % GROUP == 0

        def coded(engine, v, v0):
            at = v - OUT_LAG if FIRST <= v0 < LAST else first_coded(v0)
            return engine.value_load(e_code[0:1, bass.ds(at, 1)], min_val=0, max_val=E ** CODED - 1)

        def expert_of(code, v0, lag):
            return (code >> (3 * (v0 - lag - first_coded(v0)))) & (E - 1)

        def uses(v0, lag, i):
            return i * (GROUP // 3) + (v0 - lag) // 3

        block = stack.enter_context(nc.Block())
        out_t = out.rearrange("(t p) d -> p t d", p=P)
        y_t = y_rows[0:2 * TOKENS].rearrange("(i t p) d -> p i t d", p=P, i=2)

        def quad(k):
            return slice(BT * k, BT * k + BT)

        @block.sync
        def _(sp):
            for i in range(3):
                sp.wait_ge(y_out[i], 16 * len(range(i, SLOT_TILES, 3)))
            for k in range(BLOCKS):
                for i in range(2):
                    sp.dma_start(y_back[:, i, quad(k), :], y_t[:, i, quad(k), :]).then_inc(back_in[k], 16)
            for k in range(BLOCKS - 1):
                sp.wait_ge(result_ready, k + 1)
                sp.dma_start(out_t[:, quad(k), :], x1[:, quad(k), :]).then_inc(stored, 16)
            for i in (1, 0):
                t = slice(PAIRS - BT + i * BT // 2, PAIRS - BT + (i + 1) * BT // 2)
                sp.wait_ge(result_ready, BLOCKS + 1 - i)
                sp.dma_start(out_t[:, t, :], x1[:, t, :]).then_inc(stored, 16)
            sp.wait_ge(stored, 16 * (BLOCKS + 1))

        def scale(k):
            nc.gpsimd.wait_ge(normed_ready, k + 1)
            nc.gpsimd.tensor_tensor(scaled[:, quad(k), :], normed[:, quad(k), :],
                                    ln_w.unsqueeze(1).to_broadcast([P, BT, D]), ALU.mult).then_inc(scaled_ready, 1)

        @block.gpsimd
        def _(pool):
            g = nc.gpsimd
            g.memset(half[:], -0.5).then_inc(half_set, 1)
            pool.wait_ge(half_set, 1)
            pool.wait_ge(plane_ready, 1)
            g.tensor_tensor(in_tile[:, 2], in_tile[:, 0],
                            count16[:, 0:C].unsqueeze(2).to_broadcast([P, C, SLOT_TILES]),
                            ALU.mult).then_inc(where_pool, 1)

            pool.wait_ge(where_known, 2)

            for v in range(SLOT_TILES + OUT_LAG + 1):
                if v < SLOT_TILES:
                    r = v % GROUP
                    if v >= GROUP:
                        pool.wait_ge(y_ready, v - GROUP + 1)
                    g.indirect_dma_start(xg[r][:], None, x2_rows,
                                         bass.IndirectOffsetOnAxis(src[:, v:v + 1], 0)).then_inc(xg_in[r], 16)
                u = v - OUT_LAG - 1
                if u >= 0:
                    pool.wait_ge(y_ready, u + 1)
                    g.indirect_dma_start(y_rows, bass.IndirectOffsetOnAxis(dst[:, u:u + 1], 0),
                                         y[u % 3][:], None).then_inc(y_out[u % 3], 16)
            for k in range(BLOCKS):
                t = quad(k)
                pool.wait_ge(oveps_ready, 2 * k + 2)
                g.tensor_tensor(orstd[:, t], oveps[:, t], half[:, t], ALU.pow).then_inc(orstd_ready, 1)
                pool.wait_ge(orstd_ready, k + 1)
                g.tensor_tensor(onmr[:, t], onmean[:, t], orstd[:, t], ALU.mult).then_inc(onmr_ready, 1)
                if 1 <= k < BLOCKS - 1:
                    scale(k - 1)

        @block.vector
        def _(dve):
            v_ = nc.vector
            done = [0]

            def chained(ins):
                done[0] += 1
                ins.then_inc(route, 1)

            def all_before():
                dve.wait_ge(route, done[0])

            v_.tensor_tensor(gap[:], top[:, :, 1], top[:, :, 0], ALU.subtract).then_inc(gap_ready, 1)
            chained(v_.tensor_copy(top_f[:], top_i[:, :, 0:2]))
            all_before()
            for i in range(2):
                chained(v_.tensor_tensor(chosen[i][:], top_f[:, :, i:i + 1].to_broadcast([P, PAIRS, E]),
                                         count[:, 0:E].unsqueeze(1).to_broadcast([P, PAIRS, E]), ALU.is_equal))
            all_before()
            v_.tensor_tensor(both[:], chosen[0][:], chosen[1][:], ALU.add).then_inc(both_ready, 1)
            dve.wait_ge(ratio_ready, 1)
            chained(v_.tensor_scalar(denom[:], ratio[:], 1.0, None, ALU.add))
            all_before()
            chained(v_.reciprocal(wt[:, 0, :], denom[:]))
            all_before()
            chained(v_.tensor_tensor(wt[:, 1, :], wt[:, 0, :], ratio[:], ALU.mult))
            dve.wait_ge(slot_ps, 1)
            chained(v_.tensor_reduce(load[:], psM[:, 2, :].rearrange("p (t e) -> p e t", e=E), AX.X, ALU.add))
            all_before()
            chained(v_.tensor_tensor(fills[:], load[:].unsqueeze(2).to_broadcast([P, E, PAIRS]),
                                     mult128.unsqueeze(1).to_broadcast([P, E, PAIRS]), ALU.is_gt))
            all_before()
            chained(v_.tensor_reduce(tiles[:], fills[:], AX.X, ALU.add))
            all_before()
            chained(v_.tensor_tensor(tiles_upto[:], tiles[:].unsqueeze(1).to_broadcast([P, E, E]),
                                     upto_e.rearrange("p (a b) -> p a b", a=E), ALU.mult))
            all_before()
            chained(v_.tensor_reduce(ends[:], tiles_upto[:], AX.X, ALU.add))
            all_before()
            chained(v_.tensor_tensor(base[:], ends[:], tiles[:], ALU.subtract))
            all_before()
            chained(v_.tensor_scalar(base[:], base[:], float(P), None, ALU.mult))
            all_before()
            chained(v_.tensor_tensor(slot[:], psM[:, 1, :].rearrange("p (t e) -> p t e", e=E),
                                     base[:].unsqueeze(1).to_broadcast([P, PAIRS, E]), ALU.add))
            all_before()
            for i in range(2):
                chained(v_.tensor_tensor(slot_of[i][:], slot[:], chosen[i][:], ALU.mult))
            all_before()
            for i in range(2):
                chained(v_.tensor_reduce(pos[:, i, :], slot_of[i][:], AX.X, ALU.add))
            all_before()
            chained(v_.tensor_copy(pos_i[:], pos[:].rearrange("p i t -> p (i t)")))
            all_before()
            chained(v_.tensor_scalar(at_i[:, 0, :], pos_i[:], 7, None, ALU.logical_shift_right))
            chained(v_.tensor_scalar(at_i[:, 1, :], pos_i[:], P - 1, None, ALU.bitwise_and))
            all_before()
            chained(v_.tensor_copy(at_f[:], at_i[:]))
            all_before()
            chained(v_.tensor_tensor(in_tile[:, 0], at_f[:, 0, :].unsqueeze(2).to_broadcast([P, C, SLOT_TILES]),
                                     count16[:, 0:SLOT_TILES].unsqueeze(1).to_broadcast([P, C, SLOT_TILES]),
                                     ALU.is_equal))
            dve.wait_ge(route, done[0])
            v_.tensor_scalar(in_tile[:, 1], in_tile[:, 0], row_no, None, ALU.mult).then_inc(plane_ready, 1)
            for q in range(4):
                c = slice(q * C // 4, (q + 1) * C // 4)
                v_.tensor_tensor(in_row[:, c, :], at_f[:, 1, c].unsqueeze(2).to_broadcast([P, C // 4, P]),
                                 count16.unsqueeze(1).to_broadcast([P, C // 4, P]),
                                 ALU.is_equal).then_inc(where_ready, 1)
            dve.wait_ge(found_ps, 1)
            chained(v_.tensor_copy(found[:], psM[:, 3, 0:3 * SLOT_TILES].rearrange("p (a j) -> p a j", a=3)))
            all_before()
            chained(v_.scalar_tensor_tensor(row_of[:], found[:, 2, :], float(P), found[:, 1, :], ALU.mult, ALU.add))
            chained(v_.tensor_scalar(empty[:], found[:, 0, :], -1.0, 1.0, ALU.mult, ALU.add))
            all_before()
            chained(v_.tensor_scalar(second[:], row_of[:], float(TOKENS), float(TOKENS), ALU.is_ge, ALU.mult))
            chained(v_.tensor_tensor(empty[:], empty[:], empty_row, ALU.mult))
            all_before()
            v_.tensor_tensor(src[:], row_of[:], second[:], ALU.subtract).then_inc(where_known, 1)
            v_.tensor_tensor(dst[:], row_of[:], empty[:], ALU.add).then_inc(where_known, 1)
            chained(v_.tensor_tensor(passed[:], count[:, 0:SLOT_TILES].unsqueeze(2).to_broadcast([P, SLOT_TILES, E]),
                                     ends[:].unsqueeze(1).to_broadcast([P, SLOT_TILES, E]), ALU.is_ge))
            all_before()
            chained(v_.tensor_reduce(e_f[:], passed[:], AX.X, ALU.add))
            all_before()
            chained(v_.tensor_scalar(e_min[:], e_f[:], float(E - 1), None, ALU.min))
            all_before()
            for i in range(CODED - 1):
                first = codes[(i + 1) % 2][:] if i else e_min[:, CODED - 1:]
                ins = v_.scalar_tensor_tensor(e_code[:] if i == CODED - 2 else codes[i % 2][:], first, float(E),
                                              e_min[:, CODED - 2 - i:CODED - 2 - i + CODES], ALU.mult, ALU.add)
                if i == CODED - 2:
                    ins.then_inc(tab_ready, 1)
                else:
                    chained(ins)
                    all_before()
            dve.wait_ge(tab_ready, 1)

            code = [0]

            def step(v, v0, i):
                if 0 <= v0 - 2 < BLOCKS:
                    q = quad(v0 - 2)
                    v_.tensor_tensor(x1[:, q, :], x1[:, q, :], ln_b.unsqueeze(1).to_broadcast([P, BT, D]),
                                     ALU.add).then_inc(x1b_ready, 1)
                if asks(v0):
                    code[0] = coded(v_, v, v0)
                if runs(v0, 2):
                    r = (v0 - 2) % 3
                    dve.wait_ge(xg_ps, v - 1)
                    v_.tensor_copy(xg_hi[r][:], psX[:, 0:P]).then_inc(xghi_ready, 1)
                    dve.wait_ge(xghi_ready, v - 1)
                    v_.tensor_tensor(xg_lo[r][:], psX[:, 0:P], xg_hi[r][:], ALU.subtract).then_inc(xg_ready, 1)
                if runs(v0, 3):
                    xb = xg[(v0 - 3) % GROUP]
                    expert = expert_of(code[0], v0, 3)
                    v_.tensor_tensor(xb[:], xb[:], b2_all.rearrange("p (e d) -> p e d", e=E)[:, bass.ds(expert, 1), :]
                                     .rearrange("p a d -> p (a d)"), ALU.add).then_inc(xb_ready, 1)
                    r = v0 % 3
                    dve.wait_ge(gelu_ready, v - 2)
                    v_.tensor_copy(h_hi[r][:], h[r][:]).then_inc(hhi_ready, 1)
                    dve.wait_ge(hhi_ready, v - 2)
                    v_.tensor_tensor(h_lo[r][:], h[r][:], h_hi[r][:], ALU.subtract).then_inc(h_ready, 1)
                if runs(v0, OUT_LAG):
                    r = (v0 - OUT_LAG) % 3
                    dve.wait_ge(xb_ready, v - (OUT_LAG - 1))
                    dve.wait_ge(y_ps, v - (OUT_LAG - 1))
                    if v0 >= OUT_LAG + 3:
                        dve.wait_ge(y_out[r], uses(v0, OUT_LAG, i) * 16)
                    v_.tensor_tensor(y[r][:], psY[r][:, 0:D], xg[(v0 - OUT_LAG) % GROUP][:],
                                     ALU.add).then_inc(y_ready, 1)

            steps(dve, step, SLOT_TILES + OUT_LAG)

            def finish(k):
                if k == BLOCKS - 1:
                    dve.wait_ge(orstd_ready, BLOCKS)
                    for t in range(PAIRS - BT // 2, PAIRS):
                        v_.tensor_scalar(normed[:, t, :], mixed[:, t, :], omv[:, t, 0:1], orstd[:, t:t + 1],
                                         ALU.subtract, ALU.mult).then_inc(last_scaled, 1)
                    dve.wait_ge(last_scaled, BT // 2)
                    for i in (1, 0):
                        half_block = slice(PAIRS - BT + i * BT // 2, PAIRS - BT + (i + 1) * BT // 2)
                        if i == 0:
                            dve.wait_ge(normed_ready, BLOCKS)
                        v_.tensor_tensor(scaled[:, half_block, :], normed[:, half_block, :],
                                         ln_w.unsqueeze(1).to_broadcast([P, BT // 2, D]),
                                         ALU.mult).then_inc(last_scaled, 1)
                        dve.wait_ge(last_scaled, BT // 2 + 2 - i)
                        v_.tensor_tensor(x1[:, half_block, :], x1[:, half_block, :], scaled[:, half_block, :],
                                         ALU.add).then_inc(result_ready, 1)
                    return
                if k == BLOCKS - 2:
                    dve.wait_ge(normed_ready, k + 1)
                    v_.tensor_tensor(scaled[:, quad(k), :], normed[:, quad(k), :],
                                     ln_w.unsqueeze(1).to_broadcast([P, BT, D]), ALU.mult).then_inc(third_scaled, 1)
                    dve.wait_ge(third_scaled, 1)
                else:
                    dve.wait_ge(scaled_ready, k + 1)
                v_.tensor_tensor(x1[:, quad(k), :], x1[:, quad(k), :], scaled[:, quad(k), :],
                                 ALU.add).then_inc(result_ready, 1)

            dve.wait_ge(x1b_ready, BLOCKS)
            for k in range(BLOCKS):
                dve.wait_ge(back_in[k], 32)
                for t in range(BT * k, BT * k + BT):
                    dve.wait_ge(first_weighted, t + 1)
                    v_.scalar_tensor_tensor(mixed[:, t, :], y_back[:, 1, t, :], wt[:, 1, t:t + 1], weighted[:, t, :],
                                            ALU.mult, ALU.add).then_inc(mixed_ready, 1)
                for t in range(BT * k, BT * k + BT):
                    dve.wait_ge(mixed_ready, t + 1)
                    v_.bn_stats(oraw[:, t, :], mixed[:, t, :]).then_inc(oraw_done, 1)
                for t in range(BT * k, BT * k + BT):
                    dve.wait_ge(oraw_done, t + 1)
                    v_.bn_aggr(omv[:, t, :], oraw[:, t, :]).then_inc(omv_ready, 1)
                dve.wait_ge(omv_ready, BT * (k + 1))
                v_.tensor_scalar(oveps[:, quad(k)], omv[:, quad(k), 1], EPS_OUT, None, ALU.add).then_inc(oveps_ready, 1)
                v_.tensor_scalar(onmean[:, quad(k)], omv[:, quad(k), 0], -1.0, None, ALU.mult).then_inc(oveps_ready, 1)
                if k > 1:
                    finish(k - 2)
            finish(BLOCKS - 2)
            finish(BLOCKS - 1)

        @block.scalar
        def _(act):
            a = nc.scalar
            act.wait_ge(gap_ready, 1)
            a.activation(ratio[:], gap[:], ACT.Exp).then_inc(ratio_ready, 1)
            act.wait_ge(ratio_ready, 1)
            a.activation(table_load[:], gap[:, 0:1], ACT.Gelu)
            act.wait_ge(tab_ready, 1)

            def normalise(k):
                act.wait_ge(onmr_ready, k + 1)
                for t in range(BT * k, BT * k + (BT // 2 if k == BLOCKS - 1 else BT)):
                    last = a.activation(normed[:, t, :], mixed[:, t, :], ACT.Identity, bias=onmr[:, t:t + 1],
                                        scale=orstd[:, t:t + 1])
                last.then_inc(normed_ready, 1)

            code = [0]

            def step(v, v0, i):
                if asks(v0):
                    code[0] = coded(a, v, v0)
                if not runs(v0, 3):
                    return
                r = v0 % 3
                expert = expert_of(code[0], v0, 3)
                a.copy(b1_now[r][:], b1_sb[:, bass.ds(expert, 1), :].rearrange("p a c -> p (a c)")).then_inc(b1_ready, 1)
                act.wait_ge(b1_ready, v - 2)
                act.wait_ge(h_ps, v - 2)
                for c in range(FC):
                    last = a.activation(h[r][:, P * c:P * c + P], psH[r][:, P * c:P * c + P], ACT.Gelu,
                                        bias=b1_now[r][:, c:c + 1])
                last.then_inc(gelu_ready, 1)

            steps(act, step, SLOT_TILES + 3)
            for k in range(BLOCKS + 2):
                if k < BLOCKS:
                    act.wait_ge(back_in[k], 32)
                    for t in range(BT * k, BT * k + BT):
                        a.activation(weighted[:, t, :], y_back[:, 0, t, :], ACT.Identity,
                                     scale=wt[:, 0, t:t + 1]).then_inc(first_weighted, 1)
                if k > 1:
                    normalise(k - 2)

        @block.tensor
        def _(pe):
            t_ = nc.tensor
            pe.wait_ge(both_ready, 1)
            t_.matmul(psM[:, 1, :], before16, both[:].rearrange("p t e -> p (t e)"), start=True, stop=False)
            for t in range(PAIRS - 1):
                t_.matmul(psM[:, 1, E * (t + 1):], ones16, both[:, t:t + 1, :].to_broadcast([P, PAIRS - 1 - t, E]),
                          start=False, stop=t == PAIRS - 2)
            t_.matmul(psM[:, 2, :], ones16, both[:].rearrange("p t e -> p (t e)"),
                      start=True, stop=True).then_inc(slot_ps, 1)
            for c in range(C):
                if c == 0:
                    pe.wait_ge(where_pool, 1)
                if c % (C // 4) == 0:
                    pe.wait_ge(where_ready, 1 + c // (C // 4))
                last = t_.matmul(psM[:, 3, 0:3 * SLOT_TILES], in_row[:, c, :], in_tile[:, :, c, :],
                                 start=c == 0, stop=c == C - 1)
            last.then_inc(found_ps, 1)
            pe.wait_ge(tab_ready, 1)

            code = [0]

            def step(v, v0, i):
                if asks(v0):
                    code[0] = coded(t_, v, v0)
                if runs(v0, 2):
                    r = (v0 - 2) % 3
                    r = (v0 - 2) % GROUP
                    pe.wait_ge(xg_in[r], (i + (v0 - 2) // GROUP) * 16 + 16)
                    if v0 > 2:
                        pe.wait_ge(xg_ready, v - 2)
                    t_.transpose(psX[:, 0:P], xg[r][:], id32).then_inc(xg_ps, 1)
                if runs(v0, 3):
                    r = v0 % 3
                    expert = expert_of(code[0], v0, 3)
                    if v0 < FIRST or v0 >= LAST:
                        pe.wait_ge(xg_ready, v - 2)
                    if v0 >= 6:
                        pe.wait_ge(gelu_ready, v - 5)
                    for c in range(FC):
                        f = slice(P * c, P * c + P)
                        w1_hi = w_hi[:, bass.ds(expert * 2, 1), f].rearrange("p a f -> p (a f)")
                        w1_lo = w_lo[:, bass.ds(expert * 2, 1), f].rearrange("p a f -> p (a f)")
                        t_.matmul(psH[r][:, f], w1_hi, xg_hi[r][:], start=True, stop=False)
                        t_.matmul(psH[r][:, f], w1_hi, xg_lo[r][:], start=False, stop=False)
                        last = t_.matmul(psH[r][:, f], w1_lo, xg_hi[r][:], start=False, stop=True)
                    last.then_inc(h_ps, 1)
                if runs(v0, OUT_LAG):
                    r = (v0 - OUT_LAG) % 3
                    expert = expert_of(code[0], v0, OUT_LAG)
                    pe.wait_ge(h_ready, v - (OUT_LAG - 1))
                    if v0 >= OUT_LAG + 3:
                        pe.wait_ge(y_ready, v - (OUT_LAG + 2))
                    for c in range(FC):
                        f = slice(P * c, P * c + P)
                        w2_hi = w_hi[:, bass.ds(expert * 2 + 1, 1), f].rearrange("p a f -> p (a f)")
                        w2_lo = w_lo[:, bass.ds(expert * 2 + 1, 1), f].rearrange("p a f -> p (a f)")
                        t_.matmul(psY[r][:, 0:D], h_hi[r][:, f], w2_hi, start=c == 0, stop=False)
                        t_.matmul(psY[r][:, 0:D], h_hi[r][:, f], w2_lo, start=False, stop=False)
                        last = t_.matmul(psY[r][:, 0:D], h_lo[r][:, f], w2_hi, start=False, stop=c == FC - 1)
                    last.then_inc(y_ps, 1)

            steps(pe, step, SLOT_TILES + OUT_LAG)


def xattn_moe_kernel(nc, x, ctxT, w4, consts, bo, w_ffn, rows, cols, b1, out):
    with ExitStack() as stack:
        x1 = stack.enter_context(nc.sbuf_tensor("x1", [P, PAIRS, D], F32))
        w_hi = stack.enter_context(nc.sbuf_tensor("w_hi", [P, 2 * EXPERTS, 512], F16))
        w_lo = stack.enter_context(nc.sbuf_tensor("w_lo", [P, 2 * EXPERTS, 512], F16))
        x2_rows = nc.dram_tensor("x2_rows", (TOKENS, D), F32).ap()
        y_rows = nc.dram_tensor("y_rows", (2 * TOKENS + SLOT_TILES * P, D), F32).ap()
        x2 = stack.enter_context(nc.sbuf_tensor("x2", [P, PAIRS, D], F32))
        logits = stack.enter_context(nc.sbuf_tensor("logits", [P, PAIRS, EXPERTS], F32))
        top = stack.enter_context(nc.sbuf_tensor("top", [P, PAIRS, 8], F32))
        top_i = stack.enter_context(nc.sbuf_tensor("top_i", [P, PAIRS, 8], mybir.dt.uint32))
        consts16 = stack.enter_context(nc.sbuf_tensor("consts16", [P, 3, P], F16))
        row_sb = stack.enter_context(nc.sbuf_tensor("row_sb", [P, ROW_WIDTH], F32))
        col_sb = stack.enter_context(nc.sbuf_tensor("col_sb", [P, P + EXPERTS + P + 1 + SLOT_TILES], F32))
        b1_sb = stack.enter_context(nc.sbuf_tensor("b1_sb", [P, EXPERTS, FC], F32))
        attention(nc, x1, x2, logits, top, top_i, consts16, w_hi, w_lo, row_sb, col_sb, b1_sb, x, ctxT, w4, consts, bo, w_ffn, rows, cols,
                  b1, x2_rows)
        experts(nc, x1, x2, top, top_i, consts16, w_hi, w_lo, row_sb, col_sb, b1_sb, x2_rows, y_rows, out)


def kernel(**inputs):
    import numpy as np
    import concourse.bacc as bacc
    from concourse.bass_utils import run_bass_kernel_spmd

    d = {name: np.asarray(a) for name, a in inputs.items()}
    att = {name: d["L0_xattn_" + name] for name in ("Wq", "Wk", "Wv", "Wo", "bq", "bk", "bv", "bo")}
    ffn = {name: d["L0_ffn_" + name] for name in
           ("router_w", "router_b", "w1", "b1", "w2", "b2", "ln_w", "ln_b")}
    p = np.arange(P)
    f32 = np.float32
    eye = np.eye(P, dtype=f32)
    own_group = ((p[:, None] // HD) % 4 == np.arange(4)).astype(f32)
    own_row = (np.where(p[:, None] < 96, (p[:, None] // HD) % 4, p[:, None] - 96) == np.arange(4)).astype(f32)
    w1 = ffn["w1"].transpose(2, 0, 1)
    w2 = ffn["w2"].transpose(2, 0, 1).reshape(FC, P, EXPERTS, D).transpose(1, 2, 0, 3).reshape(P, EXPERTS, FF)
    arrays = {
        "x_rows": d["x"].reshape(TOKENS, D),
        "ctxT": d["ctx_1024"].reshape(TOKENS, D).T,
        "w4": np.stack([att[name].T for name in ("Wq", "Wk", "Wv", "Wo")], 1),
        "consts": np.concatenate([eye, own_group, own_row] + [att[b].reshape(D, 1) for b in ("bq", "bk", "bv")], 1),
        "bo": att["bo"].reshape(1, D),
        "w_ffn": np.stack([w1, w2], 2).reshape(P, 2 * EXPERTS, FF),
        "rows": np.concatenate([ffn["ln_w"], ffn["ln_b"], ffn["router_b"],
                                np.tri(EXPERTS, dtype=f32).ravel(), np.arange(PAIRS, dtype=f32) * P,
                                np.arange(P, dtype=f32), ffn["b2"].ravel()]).reshape(1, -1),
        "cols": np.concatenate([eye, ffn["router_w"].T, np.triu(np.ones((P, P), f32), 1), p[:, None].astype(f32),
                                (2 * TOKENS + p[:, None] + P * np.arange(SLOT_TILES)).astype(f32)], 1),
        "b1": ffn["b1"].reshape(EXPERTS, FC, P).transpose(2, 0, 1),
    }
    arrays = {name: np.ascontiguousarray(a) for name, a in arrays.items()}
    nc = bacc.Bacc("TRN2", target_bir_lowering=False, num_devices=1)
    args = [nc.dram_tensor(name, a.shape, mybir.dt.from_np(a.dtype), kind="ExternalInput").ap()
            for name, a in arrays.items()]
    out = nc.dram_tensor("out", (TOKENS, D), F32, kind="ExternalOutput").ap()
    xattn_moe_kernel(nc, *args, out)
    r = run_bass_kernel_spmd(nc, [arrays], core_ids=[0])
    return r.results[0]["out"].reshape(BATCH, SEQ, D)
```
